# Optimizing a Trainium2 kernel written in Bass

```python
import numpy as np
import jax
import jax.numpy as jnp

def _softmax(x, axis=-1):
    return jax.nn.softmax(x, axis=axis)

def _gelu(x):
    return jax.nn.gelu(x, approximate=True)

def _silu(x):
    return jax.nn.silu(x)

def _sigmoid(x):
    return jax.nn.sigmoid(x)

def _layernorm(x, axis=-1, eps=1e-05):
    m = jnp.mean(x, axis=axis, keepdims=True)
    v = jnp.var(x, axis=axis, keepdims=True)
    return (x - m) / jnp.sqrt(v + eps)

def _scatter_add(tgt, idx, src, axis=0):
    return tgt.at[idx].add(src)

def _segment_sum(src, seg, n):
    return jax.ops.segment_sum(src, seg, n)
kernel_name = 'mk_gnn_preln_d2_gnn_r8_c76665'

def setup_inputs(seed: int=0):
    np.random.seed(seed)
    _w = jnp.asarray

    def _rec_inputs():
        import jax
        import jax.numpy as jnp
        _gk = jax.random.key(seed)
        x = -0.000202 + 1 * jax.random.normal(jax.random.fold_in(_gk, 1), (6250, 128), jnp.float32)
        src = jax.random.randint(jax.random.fold_in(_gk, 2), (100000,), 0, 6250, jnp.int32)
        dst = jnp.minimum((6250 * jax.random.uniform(jax.random.fold_in(_gk, 3), (100000,)) ** 2.0).astype(jnp.int32), 49999)
        _o = jnp.argsort(dst, stable=True)
        src = src[_o]
        dst = dst[_o]
        edge_type_100 = jax.random.randint(jax.random.fold_in(_gk, 12), (100000,), 0, 100, jnp.int32)
        edge_type_8 = jax.random.randint(jax.random.fold_in(_gk, 13), (100000,), 0, 8, jnp.int32)
        return (x, src, dst, edge_type_100, edge_type_8)
    x, src, dst, edge_type_100, edge_type_8 = _rec_inputs()

    def _L0_gnn_setup():
        import jax, jax.numpy as jnp
        import numpy as np
        N = 6250
        E = 100000
        R = 100
        IN = 128
        OUT = 128
        HID = 512
        ALPHA = 0.2
        key = jax.random.key(seed)
        ks = jax.random.split(key, 12)
        xavier = lambda k, shp: jax.random.normal(k, shp, jnp.float32) * np.sqrt(2.0 / (shp[0] + shp[1])) * 1.414
        return {'x': jax.random.normal(ks[0], (N, IN), jnp.float32), 'relation_embeds': jax.random.normal(ks[1], (R, IN), jnp.float32), 'mlp_w1': jax.random.normal(ks[2], (IN, HID), jnp.float32) * np.sqrt(1.0 / IN), 'mlp_b1': jnp.zeros((HID,), jnp.float32), 'mlp_w2': jax.random.normal(ks[3], (HID, IN), jnp.float32) * np.sqrt(1.0 / HID), 'mlp_b2': jnp.zeros((IN,), jnp.float32), 'c_r': jnp.zeros((1, IN), jnp.float32), 'W': xavier(ks[4], (IN, OUT)), 'W_r': xavier(ks[5], (IN, OUT)), 'a': jax.random.normal(ks[6], (3 * OUT,), jnp.float32) * np.sqrt(2.0 / (1 + 3 * OUT)) * 1.414, 'edge_list': jax.random.randint(ks[7], (2, E), 0, N, jnp.int32), 'edge_type': jax.random.randint(ks[8], (E,), 0, R, jnp.int32)}
    _L0_gnn_all = _L0_gnn_setup()
    _L0_gnn_in = {k: v for k, v in _L0_gnn_all.items() if k in ('relation_embeds', 'mlp_w1', 'mlp_b1', 'mlp_w2', 'mlp_b2', 'c_r', 'W', 'W_r', 'a')}
    del _L0_gnn_all

    def _L1_gnn_setup():
        import jax, jax.numpy as jnp
        import numpy as np
        N_NODES = 6250
        N_EDGES = 62500
        IN_DIM = 128
        OUT_DIM = 128
        N_REL = 8
        key = jax.random.key(seed)
        k1, k2, k3, k4 = jax.random.split(key, 4)
        x = jax.random.normal(k1, (N_NODES, IN_DIM), dtype=jnp.float32)
        limit = float(np.sqrt(6.0 / (IN_DIM + OUT_DIM)))
        weight = jax.random.uniform(k2, (N_REL, IN_DIM, OUT_DIM), dtype=jnp.float32, minval=-limit, maxval=limit)
        bias = jnp.zeros((OUT_DIM,), dtype=jnp.float32)
        edge_index = jax.random.randint(k3, (2, N_EDGES), 0, N_NODES, dtype=jnp.int64)
        edge_type = jax.random.randint(k4, (N_EDGES,), 0, N_REL, dtype=jnp.int64)
        return {'x': x, 'weight': weight, 'bias': bias, 'edge_index': edge_index, 'edge_type': edge_type}
    _L1_gnn_all = _L1_gnn_setup()
    _L1_gnn_in = {k: v for k, v in _L1_gnn_all.items() if k in ('weight', 'bias')}
    del _L1_gnn_all
    return {'x': x, 'src': src, 'dst': dst, 'edge_type_100': edge_type_100, 'edge_type_8': edge_type_8, 'L0_gnn_relation_embeds': _L0_gnn_in['relation_embeds'], 'L0_gnn_mlp_w1': _L0_gnn_in['mlp_w1'], 'L0_gnn_mlp_b1': _L0_gnn_in['mlp_b1'], 'L0_gnn_mlp_w2': _L0_gnn_in['mlp_w2'], 'L0_gnn_mlp_b2': _L0_gnn_in['mlp_b2'], 'L0_gnn_c_r': _L0_gnn_in['c_r'], 'L0_gnn_W': _L0_gnn_in['W'], 'L0_gnn_W_r': _L0_gnn_in['W_r'], 'L0_gnn_a': _L0_gnn_in['a'], 'L1_gnn_weight': _L1_gnn_in['weight'], 'L1_gnn_bias': _L1_gnn_in['bias']}

def reference(x, src, dst, edge_type_100, edge_type_8, L0_gnn_relation_embeds, L0_gnn_mlp_w1, L0_gnn_mlp_b1, L0_gnn_mlp_w2, L0_gnn_mlp_b2, L0_gnn_c_r, L0_gnn_W, L0_gnn_W_r, L0_gnn_a, L1_gnn_weight, L1_gnn_bias):
    import jax
    import jax.numpy as jnp

    def _L0_gnn_ref(x, relation_embeds, mlp_w1, mlp_b1, mlp_w2, mlp_b2, c_r, W, W_r, a, edge_list, edge_type):
        import jax, jax.numpy as jnp
        import numpy as np
        N = 6250
        E = 100000
        R = 100
        IN = 128
        OUT = 128
        HID = 512
        ALPHA = 0.2
        src = edge_list[0]
        dst = edge_list[1]
        h_i = x[src]
        h_j = x[dst]
        r_ij = relation_embeds[edge_type]
        theta_r = jnp.maximum(r_ij @ mlp_w1 + mlp_b1, 0.0) @ mlp_w2 + mlp_b2
        h_i_r = h_i * jnp.cos(theta_r) + c_r
        Wh = x @ W
        W_h_i = Wh[src]
        W_h_j = Wh[dst]
        W_r_h_i_r = h_i_r @ W_r
        a1, a2, a3 = jnp.split(a, 3)
        score = W_h_i @ a1 + W_r_h_i_r @ a2 + W_h_j @ a3
        lrelu = jnp.where(score > 0, score, ALPHA * score)
        edge_e = jnp.exp(-lrelu)
        e_rowsum = jax.ops.segment_sum(edge_e, src, num_segments=N)[:, None]
        e_rowsum = jnp.where(e_rowsum == 0.0, 1e-12, e_rowsum)
        h_local = jax.ops.segment_sum(edge_e[:, None] * W_h_j, src, num_segments=N)
        h_local = h_local / e_rowsum
        return jax.nn.elu(h_local)

    def _L1_gnn_ref(x, weight, bias, edge_index, edge_type):
        import jax, jax.numpy as jnp
        import numpy as np
        N_NODES = 6250
        N_EDGES = 62500
        IN_DIM = 128
        OUT_DIM = 128
        N_REL = 8
        src = edge_index[0]
        dst = edge_index[1]
        xw = jnp.einsum('ni,rio->rno', x, weight)
        msgs = jax.nn.relu(xw[edge_type, src] + bias)
        out = jax.ops.segment_sum(msgs, dst, num_segments=x.shape[0])
        return out
    edge_index = jnp.stack([src, dst])
    h = jnp.maximum(_layernorm(x, axis=-1), 0.0)
    x = x + _L0_gnn_ref(h, L0_gnn_relation_embeds, L0_gnn_mlp_w1, L0_gnn_mlp_b1, L0_gnn_mlp_w2, L0_gnn_mlp_b2, L0_gnn_c_r, L0_gnn_W, L0_gnn_W_r, L0_gnn_a, edge_index, edge_type_100)
    h = jnp.maximum(_layernorm(x, axis=-1), 0.0)
    x = x + _L1_gnn_ref(h, L1_gnn_weight, L1_gnn_bias, edge_index, edge_type_8)
    return x

_drawn_inputs = setup_inputs


def setup_inputs(seed=0):
    import zlib

    import numpy as np

    out = dict(_drawn_inputs(seed))
    spreads = {'L0_gnn_mlp_b1': (0.0, 0.8),
     'L0_gnn_mlp_b2': (0.0, 2.0),
     'L0_gnn_c_r': (0.0, 2.0),
     'L1_gnn_bias': (0.0, 0.1)}
    factors = {'L0_gnn_relation_embeds': 6.407, 'L0_gnn_mlp_w1': 6.386, 'L0_gnn_mlp_w2': 6.366}
    for name, (base, spread) in spreads.items():
        noise = np.random.default_rng([zlib.crc32(name.encode()), seed]).standard_normal(out[name].shape)
        drawn = base * np.exp(spread * noise) if base else spread * noise
        out[name] = jnp.asarray(drawn.astype(out[name].dtype))
    for name, factor in factors.items():
        out[name] = (out[name] * factor).astype(out[name].dtype)
    return out
```

```python
from contextlib import ExitStack

import concourse.bass as bass
from concourse import mybir

ALU = mybir.AluOpType
ACT = mybir.ActivationFunctionType
ENG = mybir.EngineType
F32 = mybir.dt.float32
BF16 = mybir.dt.bfloat16
I32 = mybir.dt.int32
ds = bass.ds

P = 128
N, D = 6250, 128
NW = -(-N // P)
LASTN = N - (NW - 1) * P
E = 100000
EP, EC = 125, 800
R = 100
HID = 512
HK = HID // P
R8 = 8

F_DST, F_POS, F_SRC, F_TYPE, F_MSG, NF = 0, 1, 2, 3, 4, 5
C_A3, C_ONE, C_SRC, C_TYPE, ROW = 128, 129, 130, 131, 132
ACC = 130
T_S, TC, TS = 129, 229, 230
FAR = 1.0e6
OUT = 1048576.0

HB = 4
GA = 6
TURNS_A = -(-(-(-E // P) + NW) // (HB * GA))
CHUNKS_D = TURNS_A * HB * GA
QB, GB = 4, 2
CB = QB * GB
TURNS_B = -(-(-(-E // (P * QB)) + NW) // (HB * GB))
BLOCKS_S = TURNS_B * HB * GB + GB
GC, HC = 4, 3
TURNS_C = CHUNKS_D // (GC * HC)
assert TURNS_C * GC * HC == CHUNKS_D
KD = -(-CHUNKS_D // P)
KS = -(-BLOCKS_S // P)
TAIL = P * QB

TWO_PI_A = 6.28125
TWO_PI_B = 0.0019350051879882812
TWO_PI_C = 6.283185307179586 - TWO_PI_A - TWO_PI_B
PI = 3.1415925
EXP_TOP = -88.7225
ROUND = 12582912.0


def build(nc, x, src, dst, t100, t8, emb, w1, b1, w2, b2, c_r, W, W_r, a, w8, bias, out):
    with ExitStack() as ctx:
        def sb(name, shape, dt=F32):
            return ctx.enter_context(nc.sbuf_tensor(name, shape, dt))

        def sem(name):
            return ctx.enter_context(nc.semaphore(name))

        def dram(name, shape, dt=F32):
            return nc.dram_tensor(name, shape, dt, kind="Internal").ap()

        bank = [ctx.enter_context(nc.psum_tensor(f"bank{i}", [P, 512], F32)) for i in range(8)]

        rec_d = dram("rec_d", [E + TAIL, NF])
        rows_d = dram("rows_d", [E + TAIL, ROW])
        msg_d = dram("msg_d", [NW * P * R8, D])
        tabw_d = {s: dram(f"tabw_{s}", [P * k]) for s, k in (("d", KD), ("s", KS))}
        tabi_d = {s: dram(f"tabi_{s}", [2, P * k], I32) for s, k in (("d", KD), ("s", KS))}

        iota_c = sb("iota_c", [P, P])
        iota_p = sb("iota_p", [P, 1])
        iota_cb = sb("iota_cb", [P, P], BF16)
        ident = sb("ident", [P, P])
        identb = sb("identb", [P, P], BF16)
        before = sb("before", [P, P])
        ones = sb("ones", [P, P])
        ones3 = sb("ones3", [3, P], BF16)
        far = sb("far", [P, QB * ROW])
        farrec = sb("farrec", [P, QB * NF])
        chunk_no = sb("chunk_no", [P, KD + KS])

        area = sb("area", [P, EC * (NF + 13)])

        def column(n, dt=F32):
            view = area[0:EP, EC * (NF + n):EC * (NF + n + 1)]
            return view if dt == F32 else view.bitcast(dt)

        rec = area[0:EP, 0:EC * NF].rearrange("p (c f) -> p c f", f=NF)
        edge_i = {k: column(n, I32) for n, k in enumerate(("src", "dst", "t100", "t8"))}
        hi_i = column(4, I32)
        hi = {"src": column(5, BF16)[:, 0:EC], "dst": column(5, BF16)[:, EC:2 * EC]}
        mask = column(6, BF16)[:, 0:EC]
        rank = column(7)
        part = [column(8), column(9)]
        pos = {"src": column(10), "dst": column(11)}
        pos_i = column(12, I32)
        nexthi = sb("nexthi", [EP, 1], I32)
        nexthif = sb("nexthif", [EP, 1])
        cnt = {k: sb(f"cnt_{k}", [EP, NW]) for k in ("src", "dst")}
        tot = {k: sb(f"tot_{k}", [P, NW]) for k in ("src", "dst")}
        upto = {k: sb(f"upto_{k}", [P, NW]) for k in ("src", "dst")}
        base = {k: sb(f"base_{k}", [EP, NW]) for k in ("src", "dst")}
        nblk = sb("nblk", [P, NW])
        nblk_i = sb("nblk_i", [P, NW], I32)
        cumblk = sb("cumblk", [P, NW])
        padded = sb("padded", [P, NW])
        junkw = sb("junkw", [P, NW])
        wcol = sb("wcol", [P, KD])
        ocol = sb("ocol", [P, KD])
        w128 = sb("w128", [P, KD])
        wo_i = sb("wo_i", [P, 2, KD], I32)
        falls = sb("falls", [EP, 2])
        fall = sb("fall", [EP, 1])
        unsorted_i = sb("unsorted_i", [1, 1], I32)
        tab_i = {"d": sb("tab_i_d", [2, P * KD], I32), "s": sb("tab_i_s", [2, P * KS], I32)}
        tab_w = {"d": sb("tab_w_d", [P, P * KD]), "s": sb("tab_w_s", [P, P * KS])}
        idx_slot = sb("idx_slot", [EP, 1], I32)
        rec_slot = sb("rec_slot", [EP, NF])

        xs = sb("xs", [P, NW, D])
        stats = sb("stats", [P, NW, 6])
        ln_m = sb("ln_m", [P, NW])
        ln_v = sb("ln_v", [P, NW])
        ln_d = sb("ln_d", [P, NW])
        ln_r = sb("ln_r", [P, NW])
        ln_b = sb("ln_b", [P, NW])
        HR = 7
        h_t = sb("h_t", [P, HR, D])
        hT = sb("hT", [P, HR, P])
        rest = area[:, 0:HR * TS].rearrange("p (t c) -> p t c", t=HR)
        table = sb("table", [P, NW, 3, TS], BF16)
        acc = area[:, 0:NW * ACC].rearrange("p (w c) -> p w c", c=ACC)
        rinv = sb("rinv", [P, NW])
        ez = area[:, NW * ACC:NW * ACC + HR * D].rearrange("p (t c) -> p t c", t=HR)

        wsb = sb("wsb", [P, 2, P])
        emb_sb = sb("emb_sb", [R, D])
        onehots = sb("onehots", [P, HC * GC * P])
        w1_sb = onehots[:, 0:HID]
        w2_sb = onehots[:, HID:2 * HID].rearrange("p (k n) -> p k n", n=P)
        wT = onehots[:, 2 * HID:2 * HID + 2 * P + R]
        b1_sb = sb("b1_sb", [P, HK])
        b2_sb = sb("b2_sb", [P, 1])
        cr_sb = sb("cr_sb", [P, 1])
        a_sb = sb("a_sb", [P, 3])
        w8_sb = sb("w8_sb", [P, R8, P])
        bias_sb = sb("bias_sb", [1, P])
        bias3 = sb("bias3", [1, 3, P], BF16)
        biasr = sb("biasr", [1, 2, P])
        biasm = sb("biasm", [3, R8, P], BF16)
        wa = sb("wa", [P, 3])
        rhs1 = sb("rhs1", [P, TS])
        crow = sb("crow", [1, TS])

        rec_a = sb("rec_a", [P, HB, GA, NF])
        rel_a = sb("rel_a", [P, 2, GA])
        q_a = sb("q_a", [P, 2, GA])
        m_a = sb("m_a", [P, 2, GA])
        idx_a = sb("idx_a", [P, HB, GA], I32)
        one_a = sb("one_a", [P, 2, CB, P], BF16)
        early = one_a[:, :, :, :].rearrange("p h s e -> p (h s e)").bitcast(F32)
        hidT = early[:, 0:HK * R].rearrange("p (k r) -> p k r", k=HK)
        th = early[:, HK * R:(HK + 1) * R]
        whole = early[:, (HK + 1) * R:(HK + 2) * R]
        oneT_a = sb("oneT_a", [P, 2, CB, P], BF16)
        ring = NW * ACC
        rows_a = area[:, ring:ring + HB * GA * ROW].rearrange("p (h j f) -> p h j f", h=HB, j=GA)
        rows_b = area[:, ring:ring + HB * CB * ROW].rearrange("p (h b q f) -> p h b q f", h=HB, b=GB, q=QB)
        onew_b = area[:, ring + HB * CB * ROW:ring + HB * CB * ROW + 2 * CB * P].rearrange(
            "p (h s e) -> p h s e", h=2, s=CB)
        msg_c = area[:, ring:ring + HC * GC * D].rearrange("p (g j d) -> p g j d", g=HC, j=GC)
        rel_b = sb("rel_b", [P, 2, GB, QB])
        junk_b = sb("junk_b", [P, CB, R], BF16)
        sel_b = sb("sel_b", [P, 2, CB])
        sc_b = sb("sc_b", [P, 2, CB])
        lr_b = sb("lr_b", [P, 2, CB])
        wg_b = sb("wg_b", [P, 2, CB])
        rec_c = sb("rec_c", [P, HC, GC, NF])
        rel_c = sb("rel_c", [P, HC, GC])
        one_c = onehots[:, :].rearrange("p (g j e) -> p g j e", g=HC, j=GC)
        msg_o = area[:, NW * ACC:NW * ACC + HR * R8 * D].rearrange("p (t c) -> p t c", t=HR)

        edges_in = sem("edges_in")
        weights_in = sem("weights_in")
        x_in = sem("x_in")
        iotas = sem("iotas")
        consts = sem("consts")
        vstep = sem("vstep")
        pstep = sem("pstep")
        counted = sem("counted")
        totals = sem("totals")
        flag_i = sem("flag_i")
        table_made = sem("table_made")
        table_out = sem("table_out")
        tables = sem("tables")
        recs_made = sem("recs_made")
        posd_made = sem("posd_made")
        posd_step = sem("posd_step")
        part_made = sem("part_made")
        part_added = sem("part_added")
        recs_out = sem("recs_out")
        slot_out = sem("slot_out")
        tails_made = sem("tails_made")
        tails_out = sem("tails_out")
        weightsT = sem("weightsT")
        wT_copied = sem("wT_copied")
        hid_done = sem("hid_done")
        hid_copied = sem("hid_copied")
        theta_done = sem("theta_done")
        angle = sem("angle")
        cosine = sem("cosine")
        rhs_ready = sem("rhs_ready")
        bias_split = sem("bias_split")
        bias_in = sem("bias_in")
        var_ready = sem("var_ready")
        std_ready = sem("std_ready")
        ln_ready = sem("ln_ready")
        h_ready = sem("h_ready")
        h_turned = sem("h_turned")
        hT_ready = sem("hT_ready")
        dense = sem("dense")
        high = sem("high")
        rest_mid = sem("rest_mid")
        mid = sem("mid")
        low = sem("low")
        a_rec = [sem(f"a_rec{h}") for h in range(HB)]
        a_idx = [sem(f"a_idx{h}") for h in range(HB)]
        a_one = [sem(f"a_one{h}") for h in range(2)]
        a_turned = [sem(f"a_turned{h}") for h in range(2)]
        a_oneT = [sem(f"a_oneT{h}") for h in range(2)]
        a_got = [sem(f"a_got{h}") for h in range(2)]
        a_rows = [sem(f"a_rows{h}") for h in range(HB)]
        a_sent = [sem(f"a_sent{h}") for h in range(HB)]
        b_rows = [sem(f"b_rows{h}") for h in range(HB)]
        b_one = [sem(f"b_one{h}") for h in range(2)]
        b_turned = [sem(f"b_turned{h}") for h in range(2)]
        b_oneT = [sem(f"b_oneT{h}") for h in range(2)]
        b_got = [sem(f"b_got{h}") for h in range(2)]
        b_lr = [sem(f"b_lr{h}") for h in range(2)]
        b_wg = [sem(f"b_wg{h}") for h in range(2)]
        held = sem("held")
        b_onew = [sem(f"b_onew{h}") for h in range(2)]
        b_sum = [sem(f"b_sum{h}") for h in range(HB)]
        b_added = [sem(f"b_added{h}") for h in range(2)]
        z_ready = sem("z_ready")
        z_exp = sem("z_exp")
        msg_done = sem("msg_done")
        msg_half = [sem("msg_half0"), sem("msg_half1")]
        msg_out = sem("msg_out")
        c_rec = [sem(f"c_rec{g}") for g in range(HC)]
        c_one = [sem(f"c_one{g}") for g in range(HC)]
        c_msg = [sem(f"c_msg{g}") for g in range(HC)]
        c_sum = [sem(f"c_sum{g}") for g in range(HC)]
        c_added = [sem(f"c_added{g}") for g in range(HC)]
        x_done = sem("x_done")
        out_done = sem("out_done")

        def entries(engine, side, which, first, count, top):
            _, values = nc.values_load_multi_w_load_instructions(
                tab_i[side][which:which + 1, ds(first, count)], engines=[engine], min_val=0, max_val=top,
                skip_runtime_bounds_check_because="the table is clamped to 0..top where it is made")
            return values

        def part_of_table(window, k):
            return table[:, ds(window, 1), k, 0:TC].rearrange("p o c -> p (o c)")

        def since(eng, s, value):
            if not isinstance(value, int) or value > 0:
                eng.wait_ge(s, value)

        def turns(eng, count):
            def run(body):
                body(0)
                with eng.Fori(1, count) as i:
                    body(i)
            return run

        class Chain:

            def __init__(self, eng, s):
                self.eng, self.s, self.n, self.k = eng, s, 0, 0

            def link(self, ins):
                ins.then_inc(self.s, 1)
                self.k += 1
                self.eng.wait_ge(self.s, self.n + self.k)

            def turn(self, i, each, start=1):
                self.n, self.k = self.n + self.k, 0
                if not isinstance(i, int):
                    self.first, self.each, self.start = self.n, each, start
                    self.n = self.first + (i - start) * each

            def end(self, count):
                assert self.k == self.each, (self.k, self.each)
                self.n, self.k = self.first + (count - self.start) * self.each, 0

        def before2(k, i):
            return (k - 2, i + 1) if k >= 2 else (k - 2 + HB, i)

        block = ctx.enter_context(nc.Block())

        @block.sync
        def _(sp):
            for k, v in (("dst", dst), ("src", src), ("t100", t100), ("t8", t8)):
                sp.dma_start(edge_i[k][:, :], v.rearrange("(p c) -> p c", p=EP)).then_inc(edges_in, 16)
            with nc.allow_non_contiguous_dma(reason="one value of each partition's first edge"):
                sp.dma_start(nexthi[0:EP - 1, :], dst.rearrange("(p c) -> p c", p=EP)[1:EP, 0:1]).then_inc(edges_in, 16)
            sp.dma_start(wsb[:, 0, :], W).then_inc(weights_in, 16)
            sp.dma_start(wsb[:, 1, :], W_r).then_inc(weights_in, 16)
            sp.dma_start(emb_sb[:, :], emb).then_inc(weights_in, 16)
            sp.dma_start(w1_sb[:, :], w1).then_inc(weights_in, 16)
            sp.dma_start(w2_sb[:, :, :], w2.rearrange("(k p) n -> p k n", p=P)).then_inc(weights_in, 16)
            sp.dma_start(w8_sb[:, :, :], w8.rearrange("r p n -> p r n")).then_inc(weights_in, 16)
            with nc.allow_non_contiguous_dma(reason="short vectors turned onto the partitions"):
                sp.dma_start(b1_sb[:, :], b1.rearrange("(k p) -> p k", p=P)).then_inc(weights_in, 16)
                sp.dma_start(b2_sb[:, :], b2.rearrange("(p o) -> p o", o=1)).then_inc(weights_in, 16)
                sp.dma_start(cr_sb[:, :], c_r.rearrange("o p -> p o")).then_inc(weights_in, 16)
                sp.dma_start(a_sb[:, :], a.rearrange("(k p) -> p k", p=P)).then_inc(weights_in, 16)
            sp.dma_start(bias_sb[:, :], bias.rearrange("(o n) -> o n", o=1)).then_inc(weights_in, 16)
            sp.dma_start(xs[:, 0:NW - 1, :], x[0:(NW - 1) * P, :].rearrange("(w p) d -> p w d", p=P)).then_inc(x_in, 16)
            sp.wait_ge(consts, 1)
            sp.dma_start(xs[0:LASTN, NW - 1, :], x[(NW - 1) * P:N, :]).then_inc(x_in, 16)
            sp.wait_ge(tails_made, 1)
            sp.dma_start(rows_d[E:E + TAIL, :].rearrange("(p q) f -> p (q f)", p=P), far[:, :]).then_inc(tails_out, 16)
            sp.dma_start(rec_d[E:E + TAIL, :].rearrange("(p q) f -> p (q f)", p=P), farrec[:, :]).then_inc(tails_out, 16)
            sp.wait_ge(bias_split, 1)
            for k in range(3):
                sp.dma_start(biasm[k:k + 1, :, :], bias3[0:1, k:k + 1, :].to_broadcast([1, R8, P])).then_inc(bias_in, 16)
            for n, (s, k) in enumerate((("d", KD), ("s", KS))):
                sp.wait_ge(table_made, n + 1)
                sp.dma_start(tabw_d[s].rearrange("(p k) -> p k", p=P), w128[:, 0:k]).then_inc(table_out, 16)
                sp.dma_start(tabi_d[s].rearrange("t (p k) -> p t k", p=P), wo_i[:, :, 0:k]).then_inc(table_out, 16)
                sp.wait_ge(table_out, 32 * (n + 1))
                sp.dma_start(tab_i[s][:, :], tabi_d[s]).then_inc(tables, 16)
                sp.dma_start(tab_w[s][:, :], tabw_d[s].rearrange("(o c) -> o c", o=1).to_broadcast([P, P * k])).then_inc(tables, 16)
            sp.wait_ge(tables, 64)
            sp.wait_ge(tails_out, 32)

            sp.wait_ge(recs_out, 1)
            @turns(sp, TURNS_A)
            def _(i):
                for k in range(HB):
                    since(sp, a_idx[k], i)
                    o = entries(ENG.SP, "d", 0, (i * HB + k) * GA, GA, E)
                    for j in range(GA):
                        sp.dma_start(rec_a[:, k, j, :], rec_d[ds(o[j], P), :]).then_inc(a_rec[k], 16)

            for k in range(HB):
                sp.wait_ge(a_sent[k], 16 * GA * TURNS_A)

            def load_rows(i, k):
                since(sp, b_sum[k], i)
                o = entries(ENG.SP, "s", 0, (i * HB + k) * GB, GB, E)
                for b in range(GB):
                    sp.dma_start(rows_b[:, k, b, :, :], rows_d[ds(o[b], P * QB), :].rearrange(
                        "(p q) f -> p q f", q=QB)).then_inc(b_rows[k], 16)

            @turns(sp, TURNS_B)
            def _(i):
                for k in range(HB):
                    load_rows(i, k)
            load_rows(TURNS_B, 0)

            msg_v = msg_d.rearrange("(w p r) d -> p w (r d)", p=P, r=R8)
            @turns(sp, NW // HR)
            def _(i):
                for t in range(HR):
                    sp.wait_ge(msg_half[0], i * HR + t + 1)
                    sp.wait_ge(msg_half[1], i * HR + t + 1)
                    sp.dma_start(msg_v[:, ds(i * HR + t, 1), :], msg_o[:, t:t + 1, :]).then_inc(msg_out, 16)

            @turns(sp, TURNS_C)
            def _(i):
                for g in range(HC):
                    since(sp, c_msg[g], 16 * GC * i)
                    since(sp, c_one[g], i)
                    o = entries(ENG.SP, "d", 0, i * (GC * HC) + g * GC, GC, E)
                    for j in range(GC):
                        sp.dma_start(rec_c[:, g, j, :], rec_d[ds(o[j], P), :]).then_inc(c_rec[g], 16)

            sp.wait_ge(x_done, 1)
            sp.dma_start(out[0:(NW - 1) * P, :].rearrange("(w p) d -> p w d", p=P), xs[:, 0:NW - 1, :]).then_inc(out_done, 16)
            sp.dma_start(out[(NW - 1) * P:N, :], xs[0:LASTN, NW - 1, :]).then_inc(out_done, 16)
            sp.wait_ge(out_done, 32)

        @block.gpsimd
        def _(pool):
            steps = Chain(pool, pstep)
            steps.link(nc.gpsimd.memset(pos["src"][:, :], -1.0))
            nc.gpsimd.iota(iota_c[:, :], pattern=[[1, P]], base=0, channel_multiplier=0,
                           allow_small_or_imprecise_dtypes=True).then_inc(iotas, 1)
            nc.gpsimd.iota(iota_p[:, :], pattern=[[0, 1]], base=0, channel_multiplier=1,
                           allow_small_or_imprecise_dtypes=True).then_inc(iotas, 1)
            nc.gpsimd.iota(chunk_no[:, 0:KD], pattern=[[1, KD]], base=0, channel_multiplier=KD,
                           allow_small_or_imprecise_dtypes=True).then_inc(iotas, 1)
            nc.gpsimd.iota(chunk_no[:, KD:KD + KS], pattern=[[1, KS]], base=0, channel_multiplier=KS,
                           allow_small_or_imprecise_dtypes=True).then_inc(iotas, 1)
            nc.gpsimd.memset(far[:, :], FAR)
            steps.link(nc.gpsimd.memset(farrec[:, :], FAR))
            nc.gpsimd.memset(farrec[:, :].rearrange("p (q f) -> p q f", f=NF)[:, :, F_MSG], 0.0).then_inc(tails_made, 1)

            with pool.Fori(0, NW // HR) as i:
                for t in range(HR):
                    pool.wait_ge(part_made, i * HR + t + 1)
                    nc.gpsimd.tensor_tensor(pos["src"][:, :], pos["src"][:, :], part[t % 2][:, :], ALU.add).then_inc(part_added, 1)
                    pool.wait_ge(part_added, i * HR + t + 1)

            pool.wait_ge(recs_made, 1)
            pool.wait_ge(flag_i, 1)
            unsorted = nc.values_load(unsorted_i[0:1, 0:1], engines=[ENG.Pool], min_val=0, max_val=1,
                                      skip_runtime_bounds_check_because="the flag is clamped to 0..1")
            with pool.If(unsorted):
                pool.wait_ge(posd_made, 1)
                with pool.Fori(0, EC) as c:
                    nc.gpsimd.tensor_copy(idx_slot[:, :], pos_i[:, ds(c, 1)])
                    nc.gpsimd.tensor_copy(rec_slot[:, :], rec[:, ds(c, 1), :].rearrange("p c f -> p (c f)")).then_inc(pstep, 1)
                    pool.wait_ge(pstep, steps.k + 1 + c)
                    pool.sem_inc(held, 1)
                    nc.gpsimd.indirect_dma_start(
                        out=rec_d[0:E, :], out_offset=bass.IndirectOffsetOnAxis(ap=idx_slot[:, 0:1], axis=0),
                        in_=rec_slot[:, :], in_offset=None, bounds_check=E - 1, oob_is_err=False).then_inc(slot_out, 16)
                    pool.wait_ge(slot_out, 16 * (c + 1))
                    pool.sem_inc(held, 1)
            with pool.Else():
                pool.dma_start(rec_d[0:E, :].rearrange("(p c) f -> p (c f)", p=EP),
                               rec[:, :, :].rearrange("p c f -> p (c f)")).then_inc(slot_out, 16)
                pool.wait_ge(slot_out, 16)
            nc.gpsimd.memset(rows_a[:, :, :, C_ONE], 1.0)
            nc.gpsimd.memset(acc[:, :, :], 0.0).then_inc(recs_out, 1)

            @turns(pool, TURNS_A)
            def _(i):
                for k in range(HB):
                    pool.wait_ge(a_idx[k], i + 1)
                    pool.wait_ge(a_rows[k], i + 1)
                    pool.sem_inc(held, 1)
                    for j in range(GA):
                        nc.gpsimd.indirect_dma_start(
                            out=rows_d[0:E, :], out_offset=bass.IndirectOffsetOnAxis(ap=idx_a[:, k, j:j + 1], axis=0),
                            in_=rows_a[:, k, j, :], in_offset=None, bounds_check=E - 1,
                            oob_is_err=False).then_inc(a_sent[k], 16)

            @turns(pool, TURNS_B)
            def _(i):
                for k in range(HB):
                    p, n = k % 2, 2 * i + k // 2
                    slot, used = before2(k, i)
                    since(pool, b_sum[slot], used)
                    pool.wait_ge(b_wg[p], n + 1)
                    nc.gpsimd.tensor_tensor(onew_b[:, p, :, :], one_a[:, p, :, :],
                                            wg_b[:, p, :].unsqueeze(2).to_broadcast([P, CB, P]),
                                            ALU.mult).then_inc(b_onew[p], 1)

            pool.wait_ge(msg_out, 16 * NW)
            @turns(pool, TURNS_C)
            def _(i):
                for g in range(HC):
                    pool.wait_ge(c_rec[g], 16 * GC * (i + 1))
                    since(pool, c_sum[g], i)
                    pool.sem_inc(held, 1)
                    for j in range(GC):
                        nc.gpsimd.indirect_dma_start(
                            out=msg_c[:, g, j, :], out_offset=None, in_=msg_d[:, :],
                            in_offset=bass.IndirectOffsetOnAxis(ap=rec_c[:, g, j, F_MSG:F_MSG + 1].bitcast(I32), axis=0),
                            bounds_check=NW * P * R8 - 1, oob_is_err=False).then_inc(c_msg[g], 16)

        @block.vector
        def _(dve):
            v = nc.vector
            steps = Chain(dve, vstep)
            link = steps.link

            v.memset(xs[:, NW - 1, :], 0.0).then_inc(consts, 1)
            v.memset(ones[:, :], 1.0)
            v.memset(ones3[:, :], 1.0)
            v.memset(crow[:, :], 0.0)
            v.memset(rhs1[:, TC:TS], 0.0)
            v.memset(pos["dst"][:, :], -1.0)
            link(v.memset(falls[:, :], 0.0))
            dve.wait_ge(iotas, 4)
            v.tensor_scalar(before[:, :], iota_c[:, :], iota_p[:, 0:1], None, ALU.is_gt)
            v.tensor_scalar(ident[:, :], iota_c[:, :], iota_p[:, 0:1], None, ALU.is_equal)
            v.tensor_scalar(identb[:, :], iota_c[:, :], iota_p[:, 0:1], None, ALU.is_equal)
            v.tensor_copy(iota_cb[:, :], iota_c[:, :]).then_inc(consts, 1)

            dve.wait_ge(weights_in, 16 * 11)
            link(v.tensor_copy(bias3[:, 0, :], bias_sb[:, :]))
            link(v.tensor_tensor(biasr[:, 0, :], bias_sb[:, :], bias3[:, 0, :], ALU.subtract))
            link(v.tensor_copy(bias3[:, 1, :], biasr[:, 0, :]))
            link(v.tensor_tensor(biasr[:, 1, :], biasr[:, 0, :], bias3[:, 1, :], ALU.subtract))
            v.tensor_copy(bias3[:, 2, :], biasr[:, 1, :]).then_inc(bias_split, 1)

            dve.wait_ge(edges_in, 16 * 5)
            link(v.tensor_scalar(hi_i[:, :], edge_i["dst"][:, :], 7, None, ALU.arith_shift_right))
            link(v.tensor_copy(hi["dst"][:, :], hi_i[:, :]))
            link(v.tensor_scalar(hi_i[:, :], edge_i["src"][:, :], 7, None, ALU.arith_shift_right))
            link(v.tensor_copy(hi["src"][:, :], hi_i[:, :]))
            link(v.tensor_tensor(mask[:, 0:EC - 1], hi["dst"][:, 0:EC - 1], hi["dst"][:, 1:EC], ALU.is_gt))
            link(v.tensor_reduce(falls[:, 0:1], mask[:, 0:EC - 1], mybir.AxisListType.X, ALU.add))
            link(v.tensor_scalar(nexthi[0:EP - 1, :], nexthi[0:EP - 1, :], 7, None, ALU.arith_shift_right))
            link(v.tensor_copy(nexthif[0:EP - 1, :], nexthi[0:EP - 1, :]))
            link(v.tensor_tensor(falls[0:EP - 1, 1:2], hi["dst"][0:EP - 1, EC - 1:EC], nexthif[0:EP - 1, :], ALU.is_gt))
            link(v.tensor_tensor(fall[:, :], falls[:, 0:1], falls[:, 1:2], ALU.add))
            for k in ("dst", "src"):
                with dve.Fori(0, NW) as b:
                    steps.turn(b, 1, 0)
                    link(v.tensor_scalar(mask[:, :], hi[k][:, :], iota_c[0:EP, ds(b, 1)], 0.0, ALU.is_equal, ALU.add,
                                         accum_out=cnt[k][:, ds(b, 1)]))
                steps.end(NW)
            v.sem_inc(counted, 1)
            dve.wait_ge(totals, 1)
            for n, k in enumerate(("dst", "src")):
                link(v.tensor_copy(tot[k][:, :], bank[n][:, 0:NW]))
                link(v.tensor_tensor_scan(upto[k][:, :], tot[k][:, :], tot[k][:, :], 0.0, ALU.add, ALU.bypass))
                link(v.tensor_tensor(junkw[:, :], upto[k][:, :], tot[k][:, :], ALU.subtract))
                link(v.tensor_tensor(base[k][:, :], bank[n][0:EP, 64:64 + NW], junkw[0:EP, :], ALU.add))
            v.tensor_scalar(unsorted_i[:, :], bank[0][0:1, 128:129], 1.0, None, ALU.min).then_inc(flag_i, 1)
            for n, (s, k, size, kk, off) in enumerate((("d", "dst", P, KD, 0), ("s", "src", P * QB, KS, KD))):
                if n:
                    dve.wait_ge(table_out, 32)
                link(v.tensor_scalar(nblk_i[:, :], tot[k][:, :], float(size - 1), None, ALU.add))
                link(v.tensor_scalar(nblk_i[:, :], nblk_i[:, :], size.bit_length() - 1, None, ALU.arith_shift_right))
                link(v.tensor_copy(nblk[:, :], nblk_i[:, :]))
                link(v.tensor_tensor_scan(cumblk[:, :], nblk[:, :], nblk[:, :], 0.0, ALU.add, ALU.bypass))
                link(v.scalar_tensor_tensor(padded[:, :], nblk[:, :], float(size), tot[k][:, :], ALU.mult, ALU.subtract))
                for c in range(kk):
                    number = chunk_no[:, off + c:off + c + 1]
                    link(v.tensor_scalar(junkw[:, :], cumblk[:, :], number, 0.0, ALU.is_le, ALU.add,
                                         accum_out=wcol[:, c:c + 1]))
                    link(v.scalar_tensor_tensor(junkw[:, :], cumblk[:, :], number, padded[:, :], ALU.is_le, ALU.mult,
                                                accum_out=ocol[:, c:c + 1]))
                link(v.scalar_tensor_tensor(ocol[:, 0:kk], chunk_no[:, off:off + kk], float(size), ocol[:, 0:kk],
                                            ALU.mult, ALU.subtract))
                link(v.tensor_scalar(wcol[:, 0:kk], wcol[:, 0:kk], float(NW - 1), None, ALU.min))
                v.tensor_scalar(w128[:, 0:kk], wcol[:, 0:kk], float(P), None, ALU.mult)
                v.tensor_copy(wo_i[:, 1, 0:kk], wcol[:, 0:kk])
                v.tensor_scalar(wo_i[:, 0, 0:kk], ocol[:, 0:kk], float(E), None, ALU.min).then_inc(table_made, 1)

            dve.wait_ge(theta_done, 1)
            link(v.tensor_scalar(th[:, :], bank[3][:, 0:R], b2_sb[:, 0:1], None, ALU.add))
            link(v.tensor_scalar(whole[:, :], th[:, :], 0.15915494309189535, 0.25, ALU.mult, ALU.add))
            link(v.tensor_scalar(whole[:, :], whole[:, :], ROUND, None, ALU.add))
            link(v.tensor_scalar(whole[:, :], whole[:, :], ROUND, None, ALU.subtract))
            for part_of in (TWO_PI_A, TWO_PI_B, TWO_PI_C):
                link(v.scalar_tensor_tensor(th[:, :], whole[:, :], -part_of, th[:, :], ALU.mult, ALU.add))
            link(v.tensor_scalar(th[:, :], th[:, :], 1.5707963267948966, PI, ALU.add, ALU.min))
            v.tensor_scalar(th[:, :], th[:, :], -PI, None, ALU.max).then_inc(angle, 1)
            v.tensor_copy(rhs1[:, 0:D], wsb[:, 0, :])
            v.tensor_copy(rhs1[:, 128:129], wa[:, 1:2])
            v.tensor_copy(crow[:, 128:129], bank[3][0:1, 128:129])
            dve.wait_ge(cosine, 1)
            v.tensor_scalar(rhs1[:, T_S:TC], whole[:, :], wa[:, 2:3], wa[:, 0:1], ALU.mult, ALU.add).then_inc(rhs_ready, 1)

            def norm(n):
                even_m, even_v, odd_m, odd_v = (stats[:, :, c] for c in (1, 2, 4, 5))
                link(v.tensor_tensor(ln_d[:, :], even_m, odd_m, ALU.subtract))
                link(v.tensor_tensor(ln_m[:, :], even_m, odd_m, ALU.add))
                link(v.tensor_tensor(ln_v[:, :], even_v, odd_v, ALU.add))
                link(v.scalar_tensor_tensor(ln_d[:, :], ln_d[:, :], 0.25, ln_d[:, :], ALU.mult, ALU.mult))
                link(v.scalar_tensor_tensor(ln_v[:, :], ln_v[:, :], 1.0 / D, ln_d[:, :], ALU.mult, ALU.add))
                v.tensor_scalar(ln_v[:, :], ln_v[:, :], 1e-5, None, ALU.add).then_inc(var_ready, 1)
                dve.wait_ge(std_ready, n)
                link(v.reciprocal(ln_r[:, :], ln_d[:, :]))
                v.scalar_tensor_tensor(ln_b[:, :], ln_m[:, :], -0.5, ln_r[:, :], ALU.mult, ALU.mult).then_inc(ln_ready, 1)

            dve.wait_ge(x_in, 32)
            with dve.Fori(0, NW) as w:
                steps.turn(w, 1, 0)
                link(v.bn_stats(stats[:, ds(w, 1), :].rearrange("p o s -> p (o s)"),
                                xs[:, ds(w, 1), :].rearrange("p o d -> p (o d)")))
            steps.end(NW)
            norm(1)
            @turns(dve, NW // HR)
            def _(i):
                def place(t):
                    b = i * HR + t
                    link(v.tensor_scalar(mask[:, :], hi["src"][:, :], iota_c[0:EP, ds(b, 1)], None, ALU.is_equal))
                    link(v.tensor_tensor_scan(rank[:, :], mask[:, :], mask[:, :], base["src"][:, ds(b, 1)],
                                              ALU.add, ALU.max))
                    since(dve, part_added, i * HR + max(t - 1, 0))
                    v.tensor_tensor(part[t % 2][:, :], mask[:, :], rank[:, :], ALU.mult).then_inc(part_made, 1)
                    dve.wait_ge(part_made, b + 1)

                def middle(t):
                    dve.wait_ge(high, i * HR + t + 1)
                    v.tensor_tensor(rest[:, t, 0:TC], bank[2 + t % 4][:, 0:TC], part_of_table(i * HR + t, 0),
                                    ALU.subtract).then_inc(rest_mid, 1)

                def lower(t):
                    dve.wait_ge(mid, i * HR + t + 1)
                    v.tensor_tensor(part_of_table(i * HR + t, 2), rest[:, t, 0:TC], part_of_table(i * HR + t, 1),
                                    ALU.subtract).then_inc(low, 1)

                steps.turn(i, 2 * HR)
                for t in range(HR + 2):
                    if t < HR:
                        place(t)
                    if 1 <= t <= HR:
                        middle(t - 1)
                    if t >= 2:
                        lower(t - 2)
            steps.end(NW // HR)

            dve.wait_ge(low, NW)
            v.tensor_copy(rec[:, :, F_DST], edge_i["dst"][:, :])
            dve.wait_ge(part_added, NW)
            v.tensor_copy(rec[:, :, F_POS], pos["src"][:, :])
            v.tensor_copy(rec[:, :, F_SRC], edge_i["src"][:, :])
            v.tensor_copy(rec[:, :, F_TYPE], edge_i["t100"][:, :])
            v.scalar_tensor_tensor(rec[:, :, F_MSG].bitcast(I32), edge_i["src"][:, :], float(R8), edge_i["t8"][:, :],
                                   ALU.mult, ALU.add).then_inc(recs_made, 1)
            dve.wait_ge(flag_i, 1)
            unsorted = nc.values_load(unsorted_i[0:1, 0:1], engines=[ENG.DVE], min_val=0, max_val=1,
                                      skip_runtime_bounds_check_because="the flag is clamped to 0..1")
            with dve.If(unsorted):
                with dve.Fori(0, NW) as b:
                    for t, make in enumerate((
                            lambda: v.tensor_scalar(mask[:, :], hi["dst"][:, :], iota_c[0:EP, ds(b, 1)], None, ALU.is_equal),
                            lambda: v.tensor_tensor_scan(rank[:, :], mask[:, :], mask[:, :], base["dst"][:, ds(b, 1)],
                                                         ALU.add, ALU.max),
                            lambda: v.tensor_tensor(part[0][:, :], mask[:, :], rank[:, :], ALU.mult),
                            lambda: v.tensor_tensor(pos["dst"][:, :], pos["dst"][:, :], part[0][:, :], ALU.add))):
                        make().then_inc(posd_step, 1)
                        dve.wait_ge(posd_step, 4 * b + t + 1)
                v.tensor_copy(pos_i[:, :], pos["dst"][:, :]).then_inc(posd_made, 1)

            dve.wait_ge(tables, 64)
            @turns(dve, TURNS_A)
            def _(i):
                steps.turn(i, 3 * HB)
                for k in range(HB):
                    p, n = k % 2, 2 * i + k // 2
                    dve.wait_ge(a_rec[k], 16 * GA * (i + 1))
                    link(v.tensor_tensor(rel_a[:, p, :], rec_a[:, k, :, F_DST],
                                         tab_w["d"][:, ds((i * HB + k) * GA, GA)], ALU.subtract))
                    since(dve, a_turned[p], n)
                    for j in range(GA):
                        last = v.tensor_scalar(one_a[:, p, j, :], iota_cb[:, :], rel_a[:, p, j:j + 1], None, ALU.is_equal)
                    last.then_inc(a_one[p], 1)
                    link(v.scalar_tensor_tensor(q_a[:, p, :], rel_a[:, p, :], -127.0, rel_a[:, p, :], ALU.add, ALU.mult))
                    link(v.tensor_scalar(m_a[:, p, :], q_a[:, p, :], 0.0, OUT, ALU.is_gt, ALU.mult))
                    since(dve, a_sent[k], 16 * GA * i)
                    v.tensor_copy(rows_a[:, k, :, C_SRC:ROW], rec_a[:, k, :, F_SRC:F_TYPE + 1])
                    v.tensor_tensor(idx_a[:, k, :], m_a[:, p, :], rec_a[:, k, :, F_POS], ALU.add).then_inc(a_idx[k], 1)
            steps.end(TURNS_A)

            def one_hot(i, k):
                p, n = k % 2, 2 * i + k // 2
                dve.wait_ge(b_rows[k], 16 * GB * (i + 1))
                link(v.tensor_tensor(rel_b[:, p, :, :], rows_b[:, k, :, :, C_SRC],
                                     tab_w["s"][:, ds((i * HB + k) * GB, GB)].unsqueeze(2).to_broadcast([P, GB, QB]),
                                     ALU.subtract))
                since(dve, b_onew[p], n)
                for s in range(CB):
                    last = v.tensor_scalar(one_a[:, p, s, :], iota_cb[:, :], rel_b[:, p, s // QB, s % QB:s % QB + 1],
                                           None, ALU.is_equal)
                last.then_inc(b_one[p], 1)

            def score(i, k):
                p, n = k % 2, 2 * i + k // 2
                dve.wait_ge(b_got[p], n + 1)
                for s in range(CB):
                    last = v.scalar_tensor_tensor(junk_b[:, s, :], iota_c[:, 0:R], rows_b[:, k, s // QB, s % QB, C_TYPE:ROW],
                                                  bank[2 + 2 * p + s // 4][:, (s % 4) * R:(s % 4 + 1) * R],
                                                  ALU.is_equal, ALU.mult, accum_out=sel_b[:, p, s:s + 1])
                link(last)
                link(v.tensor_tensor(sc_b[:, p, :], sel_b[:, p, :],
                                     rows_b[:, k, :, :, C_A3].rearrange("p b q -> p (b q)"), ALU.add))
                link(v.scalar_tensor_tensor(lr_b[:, p, :], sc_b[:, p, :], 0.2, sc_b[:, p, :], ALU.mult, ALU.max))
                v.tensor_scalar(lr_b[:, p, :], lr_b[:, p, :], EXP_TOP, None, ALU.max).then_inc(b_lr[p], 1)

            def add_sums(i, k):
                w = entries(ENG.DVE, "s", 1, (i * HB + k) * GB, GB, NW - 1)
                dve.wait_ge(b_sum[k], i + 1)
                since(dve, b_added[(k - 1) % 2], 2 * i + (k + 1) // 2)
                for b in range(GB):
                    here = acc[:, ds(w[b], 1), :].rearrange("p o c -> p (o c)")
                    ins = v.tensor_tensor(here, here, bank[6 + k % 2][:, b * ACC:(b + 1) * ACC], ALU.add)
                    if b < GB - 1:
                        link(ins)
                ins.then_inc(b_added[k % 2], 1)

            one_hot(0, 0)

            @turns(dve, TURNS_B)
            def _(i):
                steps.turn(i, HB * (3 + GB))
                for k in range(HB):
                    one_hot(i + (k + 1) // HB, (k + 1) % HB)
                    score(i, k)
                    if k:
                        add_sums(i, k - 1)
                    elif not isinstance(i, int):
                        add_sums(i - 1, HB - 1)
            steps.end(TURNS_B)
            add_sums(TURNS_B - 1, HB - 1)
            dve.wait_ge(b_added[1], 2 * TURNS_B)

            link(v.tensor_scalar(ln_d[:, :], acc[:, :, C_ONE], 0.0, 1e-12, ALU.is_equal, ALU.mult))
            link(v.tensor_tensor(ln_d[:, :], ln_d[:, :], acc[:, :, C_ONE], ALU.add))
            link(v.reciprocal(rinv[:, :], ln_d[:, :]))
            @turns(dve, NW // HR)
            def _(i):
                steps.turn(i, 3 + HR)
                z = acc[:, ds(i * HR, HR), 0:D]
                xw = xs[:, ds(i * HR, HR), :]
                link(v.tensor_tensor(z, z, rinv[:, ds(i * HR, HR)].unsqueeze(2).to_broadcast([P, HR, D]), ALU.mult))
                v.tensor_scalar(ez[:, :, :], z, 0.0, None, ALU.min).then_inc(z_ready, 1)
                link(v.scalar_tensor_tensor(xw, z, 0.0, xw, ALU.max, ALU.add))
                dve.wait_ge(z_exp, i + 1)
                link(v.scalar_tensor_tensor(xw, ez[:, :, :], -1.0, xw, ALU.add, ALU.add))
                for t in range(HR):
                    link(v.bn_stats(stats[:, ds(i * HR + t, 1), :].rearrange("p o s -> p (o s)"),
                                    xs[:, ds(i * HR + t, 1), :].rearrange("p o d -> p (o d)")))
            steps.end(NW // HR)
            norm(2)
            @turns(dve, NW // HR)
            def _(i):
                for t in range(HR + 1):
                    if t < HR:
                        dve.wait_ge(h_turned, NW + i * HR + t + 1)
                        v.tensor_copy(hT[:, t, :], bank[t % 2][:, 0:P]).then_inc(hT_ready, 1)
                    if t >= 1:
                        dve.wait_ge(msg_done, i * HR + t)
                        since(dve, msg_out, 16 * HR * i)
                        v.tensor_scalar(msg_o[:, t - 1, 512:1024], bank[3 + 2 * ((t - 1) % 3)][:, :], 0.0, None,
                                        ALU.max).then_inc(msg_half[1], 1)

            @turns(dve, TURNS_C)
            def _(i):
                steps.turn(i, HC * (1 + GC))
                for g in range(HC):
                    dve.wait_ge(c_rec[g], 16 * GC * (i + 1))
                    link(v.tensor_tensor(rel_c[:, g, :], rec_c[:, g, :, F_DST],
                                         tab_w["d"][:, ds(i * (GC * HC) + g * GC, GC)], ALU.subtract))
                    since(dve, c_sum[g], i)
                    for j in range(GC):
                        last = v.tensor_scalar(one_c[:, g, j, :], iota_c[:, :], rel_c[:, g, j:j + 1], None, ALU.is_equal)
                    last.then_inc(c_one[g], 1)
                for g in range(HC):
                    w = entries(ENG.DVE, "d", 1, i * (GC * HC) + g * GC, GC, NW - 1)
                    dve.wait_ge(c_sum[g], i + 1)
                    for j in range(GC):
                        here = xs[:, ds(w[j], 1), :].rearrange("p o d -> p (o d)")
                        link(v.tensor_tensor(here, here, bank[g][:, j * D:(j + 1) * D], ALU.add))
                    v.sem_inc(c_added[g], 1)
            steps.end(TURNS_C)
            v.sem_inc(x_done, 1)

        @block.scalar
        def _(act):
            s = nc.scalar
            act.wait_ge(weightsT, 1)
            s.copy(wT[:, :], bank[4][:, 0:2 * P + R]).then_inc(wT_copied, 1)
            act.wait_ge(hid_done, 1)
            for k in range(HK):
                s.activation(hidT[:, k, :], bank[5][:, k * R:(k + 1) * R], ACT.Relu, bias=b1_sb[:, k:k + 1])
            s.copy(wa[:, :], bank[6][:, 0:3]).then_inc(hid_copied, 1)
            act.wait_ge(angle, 1)
            s.activation(whole[:, :], th[:, :], ACT.Sin).then_inc(cosine, 1)

            def norm_turn(n, t, i):
                since(act, h_turned, (n - 1) * NW + i * HR)
                w = i * HR + t
                s.activation(h_t[:, t, :], xs[:, ds(w, 1), :].rearrange("p o d -> p (o d)"), ACT.Relu,
                             bias=ln_b[:, ds(w, 1)], scale=ln_r[:, ds(w, 1)]).then_inc(h_ready, 1)

            act.wait_ge(var_ready, 1)
            s.activation(ln_d[:, :], ln_v[:, :], ACT.Sqrt).then_inc(std_ready, 1)
            act.wait_ge(ln_ready, 1)
            @turns(act, NW // HR)
            def _(i):
                for t in range(HR):
                    norm_turn(1, t, i)
                for t in range(HR + 2):
                    if t < HR:
                        act.wait_ge(h_turned, i * HR + t + 1)
                        s.copy(hT[:, t, :], bank[t % 2][:, 0:P]).then_inc(hT_ready, 1)
                    if 1 <= t <= HR:
                        act.wait_ge(dense, i * HR + t)
                        s.copy(part_of_table(i * HR + t - 1, 0), bank[2 + (t - 1) % 4][:, 0:TC]).then_inc(high, 1)
                    if t >= 2:
                        act.wait_ge(rest_mid, i * HR + t - 1)
                        s.copy(part_of_table(i * HR + t - 2, 1), rest[:, t - 2, 0:TC]).then_inc(mid, 1)

            act.wait_ge(low, NW)
            def copy_turned(turned, got, ready, p, n, chunks):
                act.wait_ge(turned[p], n + 1)
                since(act, got[p], n)
                s.copy(oneT_a[:, p, 0:chunks, :].rearrange("p j e -> p (j e)"),
                       bank[p][:, :].bitcast(BF16)[:, 0:chunks * P]).then_inc(ready[p], 1)

            @turns(act, TURNS_A)
            def _(i):
                for pair in range(0, HB, 2):
                    for k in (pair, pair + 1):
                        copy_turned(a_turned, a_got, a_oneT, k % 2, 2 * i + k // 2, GA)
                    for k in (pair, pair + 1):
                        p, n = k % 2, 2 * i + k // 2
                        act.wait_ge(a_got[p], n + 1)
                        since(act, a_sent[k], 16 * GA * i)
                        for b in range(2):
                            last = s.copy(rows_a[:, k, 3 * b:3 * b + 3, 0:T_S],
                                          bank[2 + 2 * p + b][:, 0:3 * T_S].rearrange("p (j c) -> p j c", j=3))
                        last.then_inc(a_rows[k], 1)

            copy_turned(b_turned, b_got, b_oneT, 0, 0, CB)

            @turns(act, TURNS_B)
            def _(i):
                for k in range(HB):
                    p, n = k % 2, 2 * i + k // 2
                    act.wait_ge(b_lr[p], n + 1)
                    since(act, b_onew[p], n)
                    s.activation(wg_b[:, p, :], lr_b[:, p, :], ACT.Exp, scale=-1.0).then_inc(b_wg[p], 1)
                    copy_turned(b_turned, b_got, b_oneT, (k + 1) % 2, 2 * i + (k + 1) // 2, CB)

            @turns(act, NW // HR)
            def _(i):
                act.wait_ge(z_ready, i + 1)
                s.activation(ez[:, :, :], ez[:, :, :], ACT.Exp).then_inc(z_exp, 1)
            act.wait_ge(var_ready, 2)
            s.activation(ln_d[:, :], ln_v[:, :], ACT.Sqrt).then_inc(std_ready, 1)
            act.wait_ge(ln_ready, 2)
            @turns(act, NW // HR)
            def _(i):
                for t in range(HR):
                    norm_turn(2, t, i)
                for t in range(HR):
                    act.wait_ge(msg_done, i * HR + t + 1)
                    since(act, msg_out, 16 * HR * i)
                    s.activation(msg_o[:, t, 0:512], bank[2 + 2 * (t % 3)][:, :], ACT.Relu).then_inc(msg_half[0], 1)

        @block.tensor
        def _(pe):
            t_ = nc.tensor

            def mm(o, l, r, start=True, stop=True):
                return t_.matmul(o, l, r, start=start, stop=stop)

            pe.wait_ge(consts, 2)
            pe.wait_ge(weights_in, 16 * 11)
            t_.transpose(bank[4][:, 0:P], wsb[:, 0, :], ident[:, :])
            t_.transpose(bank[4][:, P:2 * P], wsb[:, 1, :], ident[:, :])
            t_.transpose(bank[4][:, 2 * P:2 * P + R], emb_sb[:, :], ident[0:R, 0:R]).then_inc(weightsT, 1)
            pe.wait_ge(wT_copied, 1)
            embT = wT[:, 2 * P:2 * P + R]
            for k in range(HK):
                mm(bank[5][:, k * R:(k + 1) * R], w1_sb[:, k * P:(k + 1) * P], embT)
            mm(bank[6][:, 0:1], wT[:, 0:P], a_sb[:, 0:1])
            mm(bank[6][:, 1:2], wT[:, 0:P], a_sb[:, 2:3])
            mm(bank[6][:, 2:3], wT[:, P:2 * P], a_sb[:, 1:2]).then_inc(hid_done, 1)
            pe.wait_ge(hid_copied, 1)
            for k in range(HK):
                mm(bank[3][:, 0:R], w2_sb[:, k, :], hidT[:, k, :], k == 0, k == HK - 1)
            mm(bank[3][0:1, 128:129], cr_sb[:, :], wa[:, 2:3]).then_inc(theta_done, 1)
            pe.wait_ge(counted, 1)
            for n, k in enumerate(("dst", "src")):
                mm(bank[n][:, 0:NW], ones[0:EP, :], cnt[k][:, :])
                mm(bank[n][0:EP, 64:64 + NW], before[0:EP, 0:EP], cnt[k][:, :])
            mm(bank[0][0:1, 128:129], fall[:, :], ones[0:EP, 0:1]).then_inc(totals, 1)

            pe.wait_ge(rhs_ready, 1)
            pe.wait_ge(flag_i, 1)
            def turn_features(n, i, t):
                done = (n - 1) * NW + i * HR
                pe.wait_ge(h_ready, done + t + 1)
                since(pe, hT_ready, done + max(t - 1, 0))
                t_.transpose(bank[t % 2][:, 0:P], h_t[:, t, :], ident[:, :]).then_inc(h_turned, 1)

            @turns(pe, NW // HR)
            def _(i):
                for t in range(HR + 1):
                    if t < HR:
                        turn_features(1, i, t)
                    if t >= 1:
                        pe.wait_ge(hT_ready, i * HR + t)
                        since(pe, rest_mid, i * HR + max(t - 4, 0))
                        to = bank[2 + (t - 1) % 4][:, 0:TC]
                        mm(to, hT[:, t - 1, :], rhs1[:, 0:TC], True, False)
                        mm(to, ones[0:1, :], crow[:, 0:TC], False, True).then_inc(dense, 1)

            pe.wait_ge(low, NW)
            pe.wait_ge(tables, 64)
            def turn_one_hot(one, ready, turned, p, n, chunks):
                pe.wait_ge(one[p], n + 1)
                since(pe, ready[p], n)
                for j in range(chunks):
                    last = t_.transpose(bank[p][:, :].bitcast(BF16)[:, j * P:(j + 1) * P], one_a[:, p, j, :], identb[:, :])
                last.then_inc(turned[p], 1)

            @turns(pe, TURNS_A)
            def _(i):
                for pair in range(0, HB, 2):
                    for k in (pair, pair + 1):
                        turn_one_hot(a_one, a_oneT, a_turned, k % 2, 2 * i + k // 2, GA)
                    for k in (pair, pair + 1):
                        p, n = k % 2, 2 * i + k // 2
                        w = entries(ENG.PE, "d", 1, (i * HB + k) * GA, GA, NW - 1)
                        pe.wait_ge(a_oneT[p], n + 1)
                        slot, used = before2(k, i)
                        since(pe, a_rows[slot], used)
                        for j in range(GA):
                            to = bank[2 + 2 * p + j // 3][:, (j % 3) * T_S:(j % 3 + 1) * T_S]
                            for c in range(3):
                                last = mm(to, oneT_a[:, p, j, :], table[:, ds(w[j], 1), c, 0:T_S].rearrange(
                                    "p o c -> p (o c)"), c == 0, c == 2)
                        last.then_inc(a_got[p], 1)

            def src_scores(i, k):
                p, n = k % 2, 2 * i + k // 2
                w = entries(ENG.PE, "s", 1, (i * HB + k) * GB, GB, NW - 1)
                pe.wait_ge(b_oneT[p], n + 1)
                since(pe, b_lr[p], n)
                for j in range(CB):
                    to = bank[2 + 2 * p + j // 4][:, (j % 4) * R:(j % 4 + 1) * R]
                    for c in range(3):
                        last = mm(to, oneT_a[:, p, j, :],
                                  table[:, ds(w[j // QB], 1), c, T_S:TC].rearrange("p o c -> p (o c)"), c == 0, c == 2)
                last.then_inc(b_got[p], 1)

            def weighted_sums(i, k):
                p, n = k % 2, 2 * i + k // 2
                pe.wait_ge(b_onew[p], n + 1)
                since(pe, b_added[p], n)
                for b in range(GB):
                    for q in range(QB):
                        last = mm(bank[6 + p][:, b * ACC:(b + 1) * ACC], onew_b[:, p, b * QB + q, :],
                                  rows_b[:, k, b, q, 0:ACC], q == 0, q == QB - 1)
                last.then_inc(b_sum[k], 1)

            turn_one_hot(b_one, b_oneT, b_turned, 0, 0, CB)

            @turns(pe, TURNS_B)
            def _(i):
                for k in range(HB):
                    src_scores(i, k)
                    if k:
                        weighted_sums(i, k - 1)
                    elif not isinstance(i, int):
                        weighted_sums(i - 1, HB - 1)
                    turn_one_hot(b_one, b_oneT, b_turned, (k + 1) % 2, 2 * i + (k + 1) // 2, CB)
            weighted_sums(TURNS_B - 1, HB - 1)

            pe.wait_ge(bias_in, 16 * 3)
            w8v = w8_sb[:, :, :].rearrange("p r n -> p (r n)")
            bmv = biasm[:, :, :].rearrange("k r n -> k (r n)")
            @turns(pe, NW // HR)
            def _(i):
                for t in range(HR + 1):
                    if t < HR:
                        turn_features(2, i, t)
                    if t >= 1:
                        pe.wait_ge(hT_ready, NW + i * HR + t)
                        for c in range(2):
                            since(pe, msg_half[c], i * HR + max(t - 3, 0))
                            to = bank[2 + 2 * ((t - 1) % 3) + c][:, :]
                            mm(to, hT[:, t - 1, :], w8v[:, c * 512:(c + 1) * 512], True, False)
                            last = mm(to, ones3[:, :], bmv[:, c * 512:(c + 1) * 512], False, True)
                        last.then_inc(msg_done, 1)

            pe.wait_ge(msg_half[0], NW)
            pe.wait_ge(msg_half[1], NW)
            @turns(pe, TURNS_C)
            def _(i):
                for g in range(HC):
                    pe.wait_ge(c_one[g], i + 1)
                    pe.wait_ge(c_msg[g], 16 * GC * (i + 1))
                    since(pe, c_added[g], i)
                    for j in range(GC):
                        last = mm(bank[g][:, j * D:(j + 1) * D], one_c[:, g, j, :], msg_c[:, g, j, :])
                    last.then_inc(c_sum[g], 1)


_INS = ['x', 'src', 'dst', 'edge_type_100', 'edge_type_8', 'L0_gnn_relation_embeds', 'L0_gnn_mlp_w1', 'L0_gnn_mlp_b1',
        'L0_gnn_mlp_w2', 'L0_gnn_mlp_b2', 'L0_gnn_c_r', 'L0_gnn_W', 'L0_gnn_W_r', 'L0_gnn_a', 'L1_gnn_weight',
        'L1_gnn_bias']


def kernel(**inputs):
    import numpy as _np
    import concourse.bacc as _bacc
    from concourse import mybir as _mybir
    from concourse.bass_utils import run_bass_kernel_spmd as _run

    nc = _bacc.Bacc("TRN2", target_bir_lowering=False, num_devices=1)
    arrays, args = {}, []
    for name in _INS:
        a = _np.ascontiguousarray(inputs[name])
        arrays[f"in_{name}"] = a
        args.append(nc.dram_tensor(f"in_{name}", a.shape, _mybir.dt.from_np(a.dtype), kind="ExternalInput").ap())
    out = nc.dram_tensor("out_x", (N, D), F32, kind="ExternalOutput").ap()
    build(nc, *args, out)
    r = _run(nc, [arrays], core_ids=[0])
    return r.results[0]["out_x"]
```

```python
from contextlib import ExitStack

import concourse.bass as bass
from concourse import mybir

ALU = mybir.AluOpType
ACT = mybir.ActivationFunctionType
ENG = mybir.EngineType
F32 = mybir.dt.float32
BF16 = mybir.dt.bfloat16
I32 = mybir.dt.int32
ds = bass.ds

P = 128
N, D = 6250, 128
NW = -(-N // P)
LASTN = N - (NW - 1) * P
E = 100000
EP, EC = 125, 800
R = 100
HID = 512
HK = HID // P
R8 = 8

F_DST, F_POS, F_SRC, F_TYPE, F_MSG, NF = 0, 1, 2, 3, 4, 5
C_A3, C_ONE, C_SRC, C_TYPE, ROW = 128, 129, 130, 131, 132
ACC = 130
T_S, TC, TS = 129, 229, 230
FAR = 1.0e6
OUT = 1048576.0

HB, HS = 4, 6
GA = 4
TURNS_A = -(-(-(-E // P) + NW) // (HB * GA))
CHUNKS_D = TURNS_A * HB * GA
QB, GB = 4, 2
CB = QB * GB
TURNS_B = -(-(-(-E // (P * QB)) + NW) // (HS * GB))
BLOCKS_S = TURNS_B * HS * GB + GB
GC, HC = 4, 4
TURNS_C = CHUNKS_D // (GC * HC)
assert TURNS_C * GC * HC == CHUNKS_D
KD = -(-CHUNKS_D // P)
KS = -(-BLOCKS_S // P)
TAIL = P * QB

TWO_PI_A = 6.28125
TWO_PI_B = 0.0019350051879882812
TWO_PI_C = 6.283185307179586 - TWO_PI_A - TWO_PI_B
PI = 3.1415925
TOP = 3.4028234e38
ROUND = 12582912.0


def build(nc, x, src, dst, t100, t8, emb, w1, b1, w2, b2, c_r, W, W_r, a, w8, bias, out):
    with ExitStack() as ctx:
        def sb(name, shape, dt=F32):
            return ctx.enter_context(nc.sbuf_tensor(name, shape, dt))

        def sem(name):
            return ctx.enter_context(nc.semaphore(name))

        def dram(name, shape, dt=F32):
            return nc.dram_tensor(name, shape, dt, kind="Internal").ap()

        bank = [ctx.enter_context(nc.psum_tensor(f"bank{i}", [P, 512], F32)) for i in range(8)]

        rec_d = dram("rec_d", [E + TAIL, NF])
        rows_d = dram("rows_d", [E + TAIL, ROW])
        msg_d = dram("msg_d", [NW * P * R8, D])
        tabw_d = {s: dram(f"tabw_{s}", [P * k]) for s, k in (("d", KD), ("s", KS))}
        tabi_d = {s: dram(f"tabi_{s}", [2, P * k], I32) for s, k in (("d", KD), ("s", KS))}

        iota_c = sb("iota_c", [P, P])
        iota_p = sb("iota_p", [P, 1])
        iota_cb = sb("iota_cb", [P, P], BF16)
        ident = sb("ident", [P, P])
        identb = sb("identb", [P, P], BF16)
        before = sb("before", [P, P])
        ones = sb("ones", [P, P])
        farrec = sb("farrec", [P, QB * NF])
        chunk_no = sb("chunk_no", [P, KD + KS])

        area = sb("area", [P, NW * ACC + HS * CB * ROW + 2 * CB * P])

        def column(n, dt=F32):
            view = area[0:EP, EC * (NF + n):EC * (NF + n + 1)]
            return view if dt == F32 else view.bitcast(dt)

        rec = area[0:EP, 0:EC * NF].rearrange("p (c f) -> p c f", f=NF)
        edge_i = {k: column(n, I32) for n, k in enumerate(("src", "dst", "t100", "t8"))}
        hi_i = column(4, I32)
        hi = {"src": column(5, BF16)[:, 0:EC], "dst": column(5, BF16)[:, EC:2 * EC]}
        mask = column(6, BF16)[:, 0:EC]
        rank = column(7)
        part = [column(8), column(9)]
        pos = {"dst": column(11)}
        pos_i = column(12, I32)
        unread = [column(n, BF16)[:, f:f + EC] for n in (7, 8, 9, 12) for f in (0, EC)]
        nexthi = sb("nexthi", [EP, 1], I32)
        nexthif = sb("nexthif", [EP, 1])
        cnt = {k: sb(f"cnt_{k}", [EP, NW]) for k in ("src", "dst")}
        tot = {k: sb(f"tot_{k}", [P, NW]) for k in ("src", "dst")}
        upto = {k: sb(f"upto_{k}", [P, NW]) for k in ("src", "dst")}
        base = {k: sb(f"base_{k}", [EP, NW]) for k in ("src", "dst")}
        signs = sb("signs", [EP, NW + 1])
        halves = sb("halves", [EP, NW])
        nblk = sb("nblk", [P, NW])
        nblk_i = sb("nblk_i", [P, NW], I32)
        cumblk = sb("cumblk", [P, NW])
        padded = sb("padded", [P, NW])
        junkw = sb("junkw", [P, NW])
        wcol = sb("wcol", [P, KD])
        ocol = sb("ocol", [P, KD])
        w128 = sb("w128", [P, KD])
        wo_i = sb("wo_i", [P, 2, KD], I32)
        falls = sb("falls", [EP, 2])
        fall = sb("fall", [EP, 1])
        unsorted_i = sb("unsorted_i", [1, 1], I32)
        tab_i = {"d": sb("tab_i_d", [2, P * KD], I32), "s": sb("tab_i_s", [2, P * KS], I32)}
        tab_w = {"d": sb("tab_w_d", [P, P * KD]), "s": sb("tab_w_s", [P, P * KS])}
        idx_slot = sb("idx_slot", [EP, 1], I32)
        rec_slot = sb("rec_slot", [EP, NF])

        xs = sb("xs", [P, NW, D])
        stats = sb("stats", [P, NW, 6])
        ln_m = sb("ln_m", [P, NW])
        ln_v = sb("ln_v", [P, NW])
        ln_d = sb("ln_d", [P, NW])
        ln_r = sb("ln_r", [P, NW])
        ln_b = sb("ln_b", [P, NW])
        HR = 7
        h_t = sb("h_t", [P, HR, D])
        hT = sb("hT", [P, HR, P])
        rest = area[:, EC * (NF + 11):EC * (NF + 11) + HR * TS].rearrange("p (t c) -> p t c", t=HR)
        table = sb("table", [P, NW, 3, TS], BF16)
        table_flat = table[:, :, :, :].rearrange("p w k c -> p (w k c)")
        signs_out = table_flat[0:EP, 0:HR * EC].rearrange("p (t c) -> p t c", t=HR)
        far = table_flat[:, HR * EC:HR * EC + 2 * QB * ROW].bitcast(F32)
        acc = area[:, 0:NW * ACC].rearrange("p (w c) -> p w c", c=ACC)
        rinv = sb("rinv", [P, NW])
        ez = area[:, NW * ACC:NW * ACC + HR * D].rearrange("p (t c) -> p t c", t=HR)

        wsb = sb("wsb", [P, 2, P])
        emb_sb = sb("emb_sb", [R, D])
        onehots = sb("onehots", [P, HC * GC * P])
        w1_sb = onehots[:, 0:HID]
        w2_sb = onehots[:, HID:2 * HID].rearrange("p (k n) -> p k n", n=P)
        wT = onehots[:, 2 * HID:2 * HID + 2 * P + R]
        b1_sb = sb("b1_sb", [P, HK])
        b2_sb = sb("b2_sb", [P, 1])
        cr_sb = sb("cr_sb", [P, 1])
        a_sb = sb("a_sb", [P, 3])
        w8_sb = sb("w8_sb", [P, R8, P])
        bias_sb = sb("bias_sb", [P, P])
        wa = sb("wa", [P, 3])
        xn = area[:, NW * ACC + HR * D:NW * ACC + 2 * HR * D].rearrange("p (t c) -> p t c", t=HR)
        xn_stats = sb("xn_stats", [P, HR, 6])
        rhs1 = sb("rhs1", [P, TS])
        crow = sb("crow", [1, TS])

        rec_a = sb("rec_a", [P, HB, GA, NF])
        rel_a = sb("rel_a", [P, 2, GA])
        q_a = sb("q_a", [P, 2, GA])
        m_a = sb("m_a", [P, 2, GA])
        idx_a = sb("idx_a", [P, HB, GA], I32)
        one_a = sb("one_a", [P, HS, CB, P], BF16)
        early = one_a[:, :, :, :].rearrange("p h s e -> p (h s e)").bitcast(F32)
        hidT = early[:, 0:HK * R].rearrange("p (k r) -> p k r", k=HK)
        th = early[:, HK * R:(HK + 1) * R]
        whole = early[:, (HK + 1) * R:(HK + 2) * R]
        oneT_a = sb("oneT_a", [P, 2, CB, P], BF16)
        ring = NW * ACC
        rows_a = area[:, ring:ring + HB * GA * ROW].rearrange("p (h j f) -> p h j f", h=HB, j=GA)
        rows_b = area[:, ring:ring + HS * CB * ROW].rearrange("p (h b q f) -> p h b q f", h=HS, b=GB, q=QB)
        onew_b = area[:, ring + HS * CB * ROW:ring + HS * CB * ROW + 2 * CB * P].rearrange(
            "p (h s e) -> p h s e", h=2, s=CB)
        msg_c = area[:, ring:ring + HC * GC * D].rearrange("p (g j d) -> p g j d", g=HC, j=GC)
        near_b = sb("near_b", [P, HS * GB])
        rel_b = sb("rel_b", [P, 2, GB, QB])
        junk_b = onehots[:, 2 * GB * ACC:2 * GB * ACC + CB * R // 2].bitcast(BF16).rearrange("p (s r) -> p s r", s=CB)
        sel_b = sb("sel_b", [P, 2, CB])
        sc_b = sb("sc_b", [P, 2, CB])
        lr_b = sb("lr_b", [P, 2, CB])
        wg_b = sb("wg_b", [P, 2, CB])
        cap_b = sb("cap_b", [P, 2, CB])
        rec_c = sb("rec_c", [P, HC, GC, NF])
        rel_c = sb("rel_c", [P, HC, GC])
        sums_b = onehots[:, 0:2 * GB * ACC].rearrange("p (h c) -> p h c", h=2)
        one_c = onehots[:, :].rearrange("p (g j e) -> p g j e", g=HC, j=GC)
        msg_o = area[:, NW * ACC:NW * ACC + HR * R8 * D].rearrange("p (t c) -> p t c", t=HR)

        edges_in = sem("edges_in")
        weights_in = sem("weights_in")
        x_in = sem("x_in")
        iotas = sem("iotas")
        consts = sem("consts")
        vstep = sem("vstep")
        pstep = sem("pstep")
        counted = sem("counted")
        totals = sem("totals")
        flag_i = sem("flag_i")
        table_made = sem("table_made")
        table_out = sem("table_out")
        tables = sem("tables")
        recs_made = sem("recs_made")
        posd_made = sem("posd_made")
        posd_step = sem("posd_step")
        posd_cleared = sem("posd_cleared")
        signs_made = sem("signs_made")
        halves_made = sem("halves_made")
        hi_made = sem("hi_made")
        part_made = sem("part_made")
        part_added = sem("part_added")
        recs_out = sem("recs_out")
        slot_out = sem("slot_out")
        tails_made = sem("tails_made")
        tails_out = sem("tails_out")
        weightsT = sem("weightsT")
        wT_copied = sem("wT_copied")
        hid_done = sem("hid_done")
        hid_copied = sem("hid_copied")
        theta_done = sem("theta_done")
        angle = sem("angle")
        cosine = sem("cosine")
        rhs_ready = sem("rhs_ready")
        var_ready = sem("var_ready")
        std_ready = sem("std_ready")
        ln_ready = sem("ln_ready")
        h_ready = sem("h_ready")
        h_turned = sem("h_turned")
        hT_ready = sem("hT_ready")
        dense = sem("dense")
        high = sem("high")
        rest_mid = sem("rest_mid")
        mid = sem("mid")
        low = sem("low")
        a_rec = [sem(f"a_rec{h}") for h in range(HB)]
        a_idx = [sem(f"a_idx{h}") for h in range(HB)]
        a_one = [sem(f"a_one{h}") for h in range(2)]
        a_turned = [sem(f"a_turned{h}") for h in range(2)]
        a_oneT = [sem(f"a_oneT{h}") for h in range(2)]
        a_got = [sem(f"a_got{h}") for h in range(2)]
        a_rows = [sem(f"a_rows{h}") for h in range(HB)]
        a_sent = [sem(f"a_sent{h}") for h in range(HB)]
        b_rows = [sem(f"b_rows{h}") for h in range(HS)]
        b_one = [sem(f"b_one{h}") for h in range(2)]
        b_turned = [sem(f"b_turned{h}") for h in range(2)]
        b_oneT = [sem(f"b_oneT{h}") for h in range(2)]
        b_got = [sem(f"b_got{h}") for h in range(2)]
        b_lr = [sem(f"b_lr{h}") for h in range(2)]
        b_cap = [sem(f"b_cap{h}") for h in range(2)]
        b_wg = [sem(f"b_wg{h}") for h in range(2)]
        held = sem("held")
        b_onew = [sem(f"b_onew{h}") for h in range(HS)]
        b_sum = [sem(f"b_sum{h}") for h in range(HS)]
        b_out = [sem(f"b_out{h}") for h in range(2)]
        b_half = sem("b_half")
        b_added = [sem(f"b_added{h}") for h in range(2)]
        z_ready = sem("z_ready")
        z_exp = sem("z_exp")
        z_down = sem("z_down")
        x_new = sem("x_new")
        x_kept = sem("x_kept")
        msg_done = sem("msg_done")
        msg_sum = sem("msg_sum")
        msg_ready = sem("msg_ready")
        msg_out = [sem(f"msg_out{t}") for t in range(HR)]
        c_rec = [sem(f"c_rec{g}") for g in range(HC)]
        c_one = [sem(f"c_one{g}") for g in range(HC)]
        c_msg = [sem(f"c_msg{g}") for g in range(HC)]
        c_sum = [sem(f"c_sum{g}") for g in range(HC)]
        c_added = [sem(f"c_added{g}") for g in range(HC)]
        x_done = sem("x_done")
        out_done = sem("out_done")

        def entries(engine, side, which, first, count, top):
            _, values = nc.values_load_multi_w_load_instructions(
                tab_i[side][which:which + 1, ds(first, count)], engines=[engine], min_val=0, max_val=top,
                skip_runtime_bounds_check_because="the table is clamped to 0..top where it is made")
            return values

        def part_of_table(window, k):
            return table[:, ds(window, 1), k, 0:TC].rearrange("p o c -> p (o c)")

        def since(eng, s, value):
            if not isinstance(value, int) or value > 0:
                eng.wait_ge(s, value)

        def turns(eng, count):
            def run(body):
                body(0)
                with eng.Fori(1, count) as i:
                    body(i)
            return run

        class Chain:

            def __init__(self, eng, s):
                self.eng, self.s, self.n, self.k = eng, s, 0, 0

            def link(self, ins):
                ins.then_inc(self.s, 1)
                self.k += 1
                self.eng.wait_ge(self.s, self.n + self.k)

            def put(self, ins):
                ins.then_inc(self.s, 1)
                self.k += 1
                return self.n + self.k

            def after(self, value):
                self.eng.wait_ge(self.s, value)

            def turn(self, i, each, start=1):
                self.n, self.k = self.n + self.k, 0
                if not isinstance(i, int):
                    self.first, self.each, self.start = self.n, each, start
                    self.n = self.first + (i - start) * each

            def end(self, count):
                assert self.k == self.each, (self.k, self.each)
                self.n, self.k = self.first + (count - self.start) * self.each, 0

        def before2(k, i, slots=HB):
            return (k - 2, i + 1) if k >= 2 else (k - 2 + slots, i)

        block = ctx.enter_context(nc.Block())

        @block.sync
        def _(sp):
            for k, v in (("dst", dst), ("src", src), ("t100", t100), ("t8", t8)):
                sp.dma_start(edge_i[k][:, :], v.rearrange("(p c) -> p c", p=EP)).then_inc(edges_in, 16)
            with nc.allow_non_contiguous_dma(reason="one value of each partition's first edge"):
                sp.dma_start(nexthi[0:EP - 1, :], dst.rearrange("(p c) -> p c", p=EP)[1:EP, 0:1]).then_inc(edges_in, 16)
            sp.dma_start(wsb[:, 0, :], W).then_inc(weights_in, 16)
            sp.dma_start(wsb[:, 1, :], W_r).then_inc(weights_in, 16)
            sp.dma_start(emb_sb[:, :], emb).then_inc(weights_in, 16)
            sp.dma_start(w1_sb[:, :], w1).then_inc(weights_in, 16)
            sp.dma_start(w2_sb[:, :, :], w2.rearrange("(k p) n -> p k n", p=P)).then_inc(weights_in, 16)
            sp.dma_start(w8_sb[:, :, :], w8.rearrange("r p n -> p r n")).then_inc(weights_in, 16)
            with nc.allow_non_contiguous_dma(reason="short vectors turned onto the partitions"):
                sp.dma_start(b1_sb[:, :], b1.rearrange("(k p) -> p k", p=P)).then_inc(weights_in, 16)
                sp.dma_start(b2_sb[:, :], b2.rearrange("(p o) -> p o", o=1)).then_inc(weights_in, 16)
                sp.dma_start(cr_sb[:, :], c_r.rearrange("o p -> p o")).then_inc(weights_in, 16)
                sp.dma_start(a_sb[:, :], a.rearrange("(k p) -> p k", p=P)).then_inc(weights_in, 16)
            sp.dma_start(bias_sb[:, :], bias.rearrange("(o n) -> o n", o=1).to_broadcast([P, P])).then_inc(weights_in, 16)
            sp.dma_start(xs[:, 0:NW - 1, :], x[0:(NW - 1) * P, :].rearrange("(w p) d -> p w d", p=P)).then_inc(x_in, 16)
            sp.wait_ge(consts, 1)
            sp.dma_start(xs[0:LASTN, NW - 1, :], x[(NW - 1) * P:N, :]).then_inc(x_in, 16)
            sp.wait_ge(tails_made, 1)
            sp.dma_start(rows_d[E:E + TAIL, :].rearrange("(p q) f -> p (q f)", p=P), far[:, :]).then_inc(tails_out, 16)
            sp.dma_start(rec_d[E:E + TAIL, :].rearrange("(p q) f -> p (q f)", p=P), farrec[:, :]).then_inc(tails_out, 16)
            for n, (s, k) in enumerate((("d", KD), ("s", KS))):
                sp.wait_ge(table_made, n + 1)
                sp.dma_start(tabw_d[s].rearrange("(p k) -> p k", p=P), w128[:, 0:k]).then_inc(table_out, 16)
                sp.dma_start(tabi_d[s].rearrange("t (p k) -> p t k", p=P), wo_i[:, :, 0:k]).then_inc(table_out, 16)
                sp.wait_ge(table_out, 32 * (n + 1))
                sp.dma_start(tab_i[s][:, :], tabi_d[s]).then_inc(tables, 16)
                sp.dma_start(tab_w[s][:, :], tabw_d[s].rearrange("(o c) -> o c", o=1).to_broadcast([P, P * k])).then_inc(tables, 16)
            sp.wait_ge(tables, 64)
            sp.wait_ge(tails_out, 32)

            sp.wait_ge(recs_out, 1)
            @turns(sp, TURNS_A)
            def _(i):
                for k in range(HB):
                    since(sp, a_idx[k], i)
                    o = entries(ENG.SP, "d", 0, (i * HB + k) * GA, GA, E)
                    for j in range(GA):
                        sp.dma_start(rec_a[:, k, j, :], rec_d[ds(o[j], P), :]).then_inc(a_rec[k], 16)

            for k in range(HB):
                sp.wait_ge(a_sent[k], 16 * GA * TURNS_A)

            def load_rows(i, k):
                since(sp, b_sum[k], i)
                o = entries(ENG.SP, "s", 0, (i * HS + k) * GB, GB, E)
                for b in range(GB):
                    sp.dma_start(rows_b[:, k, b, :, :], rows_d[ds(o[b], P * QB), :].rearrange(
                        "(p q) f -> p q f", q=QB)).then_inc(b_rows[k], 16)

            @turns(sp, TURNS_B)
            def _(i):
                for k in range(HS):
                    load_rows(i, k)
            load_rows(TURNS_B, 0)

            msg_v = msg_d.rearrange("(w p r) d -> p w (r d)", p=P, r=R8)
            @turns(sp, NW // HR)
            def _(i):
                for t in range(HR):
                    sp.wait_ge(msg_ready, i * HR + t + 1)
                    sp.dma_start(msg_v[:, ds(i * HR + t, 1), :], msg_o[:, t:t + 1, :]).then_inc(msg_out[t], 16)

            @turns(sp, TURNS_C)
            def _(i):
                for g in range(HC):
                    since(sp, c_msg[g], 16 * GC * i)
                    since(sp, c_one[g], i)
                    o = entries(ENG.SP, "d", 0, i * (GC * HC) + g * GC, GC, E)
                    for j in range(GC):
                        sp.dma_start(rec_c[:, g, j, :], rec_d[ds(o[j], P), :]).then_inc(c_rec[g], 16)

            sp.wait_ge(x_done, 1)
            sp.dma_start(out[0:(NW - 1) * P, :].rearrange("(w p) d -> p w d", p=P), xs[:, 0:NW - 1, :]).then_inc(out_done, 16)
            sp.dma_start(out[(NW - 1) * P:N, :], xs[0:LASTN, NW - 1, :]).then_inc(out_done, 16)
            sp.wait_ge(out_done, 32)

        @block.gpsimd
        def _(pool):
            steps = Chain(pool, pstep)
            steps.link(nc.gpsimd.memset(rec[:, :, F_POS], -1.0))
            nc.gpsimd.iota(iota_c[:, :], pattern=[[1, P]], base=0, channel_multiplier=0,
                           allow_small_or_imprecise_dtypes=True).then_inc(iotas, 1)
            nc.gpsimd.iota(iota_p[:, :], pattern=[[0, 1]], base=0, channel_multiplier=1,
                           allow_small_or_imprecise_dtypes=True).then_inc(iotas, 1)
            nc.gpsimd.iota(chunk_no[:, 0:KD], pattern=[[1, KD]], base=0, channel_multiplier=KD,
                           allow_small_or_imprecise_dtypes=True).then_inc(iotas, 1)
            nc.gpsimd.iota(chunk_no[:, KD:KD + KS], pattern=[[1, KS]], base=0, channel_multiplier=KS,
                           allow_small_or_imprecise_dtypes=True).then_inc(iotas, 1)
            nc.gpsimd.memset(far[:, :], FAR)
            steps.link(nc.gpsimd.memset(farrec[:, :], FAR))
            nc.gpsimd.memset(farrec[:, :].rearrange("p (q f) -> p q f", f=NF)[:, :, F_MSG], 0.0).then_inc(tails_made, 1)

            with pool.Fori(0, NW // HR) as i:
                for t in range(HR):
                    pool.wait_ge(part_made, i * HR + t + 1)
                    nc.gpsimd.tensor_tensor(rec[:, :, F_POS], rec[:, :, F_POS], part[t % 2][:, :], ALU.add).then_inc(part_added, 1)
                    pool.wait_ge(mid, i * HR + t + 1)
                    nc.gpsimd.tensor_tensor(part_of_table(i * HR + t, 2), rest[:, t, 0:TC], part_of_table(i * HR + t, 1),
                                            ALU.subtract).then_inc(low, 1)
                    pool.wait_ge(part_added, i * HR + t + 1)

            pool.wait_ge(recs_made, 1)
            pool.wait_ge(flag_i, 1)
            unsorted = nc.values_load(unsorted_i[0:1, 0:1], engines=[ENG.Pool], min_val=0, max_val=1,
                                      skip_runtime_bounds_check_because="the flag is clamped to 0..1")
            with pool.If(unsorted):
                pool.wait_ge(posd_made, 1)
                with pool.Fori(0, EC) as c:
                    nc.gpsimd.tensor_copy(idx_slot[:, :], pos_i[:, ds(c, 1)])
                    nc.gpsimd.tensor_copy(rec_slot[:, :], rec[:, ds(c, 1), :].rearrange("p c f -> p (c f)")).then_inc(pstep, 1)
                    pool.wait_ge(pstep, steps.k + 1 + c)
                    pool.sem_inc(held, 1)
                    nc.gpsimd.indirect_dma_start(
                        out=rec_d[0:E, :], out_offset=bass.IndirectOffsetOnAxis(ap=idx_slot[:, 0:1], axis=0),
                        in_=rec_slot[:, :], in_offset=None, bounds_check=E - 1, oob_is_err=False).then_inc(slot_out, 16)
                    pool.wait_ge(slot_out, 16 * (c + 1))
                    pool.sem_inc(held, 1)
            with pool.Else():
                pool.dma_start(rec_d[0:E, :].rearrange("(p c) f -> p (c f)", p=EP),
                               rec[:, :, :].rearrange("p c f -> p (c f)")).then_inc(slot_out, 16)
                pool.wait_ge(slot_out, 16)
            nc.gpsimd.memset(rows_a[:, :, :, C_ONE], 1.0).then_inc(recs_out, 1)
            nc.gpsimd.memset(acc[:, :, :], 0.0)

            @turns(pool, TURNS_A)
            def _(i):
                for k in range(HB):
                    pool.wait_ge(a_idx[k], i + 1)
                    pool.wait_ge(a_rows[k], i + 1)
                    pool.sem_inc(held, 1)
                    for j in range(GA):
                        nc.gpsimd.indirect_dma_start(
                            out=rows_d[0:E, :], out_offset=bass.IndirectOffsetOnAxis(ap=idx_a[:, k, j:j + 1], axis=0),
                            in_=rows_a[:, k, j, :], in_offset=None, bounds_check=E - 1,
                            oob_is_err=False).then_inc(a_sent[k], 16)

            def windows_of(first, groups):
                return entries(ENG.Pool, "s", 1, first * GB, groups * GB, NW - 1)

            def add_sums(i, k, w):
                pool.wait_ge(b_out[k % 2], HS // 2 * i + k // 2 + 1)
                since(pool, b_added[(k - 1) % 2], HS // 2 * i + (k + 1) // 2)
                pool.sem_inc(held, 1)
                for b in range(GB):
                    if b:
                        pool.wait_ge(b_half, (i * HS + k) * (GB - 1) + b)
                        pool.sem_inc(held, 1)
                    here = acc[:, ds(w[b], 1), :].rearrange("p o c -> p (o c)")
                    nc.gpsimd.tensor_tensor(here, here, sums_b[:, k % 2, b * ACC:(b + 1) * ACC], ALU.add).then_inc(
                        b_half if b < GB - 1 else b_added[k % 2], 1)

            @turns(pool, TURNS_B)
            def _(i):
                straight = isinstance(i, int)
                w = [None] * (3 * GB) + list(windows_of(0, HS - 3)) if straight else windows_of(i * HS - 3, HS)
                for k in range(HS):
                    if k >= 3:
                        add_sums(i, k - 3, w[k * GB:(k + 1) * GB])
                    elif not straight:
                        add_sums(i - 1, k + HS - 3, w[k * GB:(k + 1) * GB])
                    p, n = k % 2, HS // 2 * i + k // 2
                    slot, used = before2(k, i, HS)
                    since(pool, b_sum[slot], used)
                    pool.wait_ge(b_wg[p], n + 1)
                    pool.sem_inc(held, 1)
                    nc.gpsimd.tensor_scalar(cap_b[:, p, :], wg_b[:, p, :], TOP, None, ALU.min).then_inc(b_cap[p], 1)
                    pool.wait_ge(b_cap[p], n + 1)
                    nc.gpsimd.tensor_tensor(onew_b[:, p, :, :], one_a[:, k, :, :],
                                            cap_b[:, p, :].unsqueeze(2).to_broadcast([P, CB, P]),
                                            ALU.mult).then_inc(b_onew[k], 1)

            w = windows_of(TURNS_B * HS - 3, 3)
            for k in range(3):
                add_sums(TURNS_B - 1, HS - 3 + k, w[k * GB:(k + 1) * GB])

            for t in range(HR):
                pool.wait_ge(msg_out[t], 16 * (NW // HR))
            @turns(pool, TURNS_C)
            def _(i):
                for g in range(HC):
                    pool.wait_ge(c_rec[g], 16 * GC * (i + 1))
                    since(pool, c_sum[g], i)
                    pool.sem_inc(held, 1)
                    for j in range(GC):
                        nc.gpsimd.indirect_dma_start(
                            out=msg_c[:, g, j, :], out_offset=None, in_=msg_d[:, :],
                            in_offset=bass.IndirectOffsetOnAxis(ap=rec_c[:, g, j, F_MSG:F_MSG + 1].bitcast(I32), axis=0),
                            bounds_check=NW * P * R8 - 1, oob_is_err=False).then_inc(c_msg[g], 16)

        @block.vector
        def _(dve):
            v = nc.vector
            steps = Chain(dve, vstep)
            link = steps.link

            v.memset(xs[:, NW - 1, :], 0.0).then_inc(consts, 1)
            v.memset(ones[:, :], 1.0)
            v.memset(crow[:, :], 0.0)
            v.memset(rhs1[:, TC:TS], 0.0)
            v.memset(signs[:, NW:NW + 1], -float(EC))
            link(v.memset(falls[:, :], 0.0))
            dve.wait_ge(iotas, 4)
            v.tensor_scalar(halves[:, :], iota_c[0:EP, 0:NW], -1.0, 0.5, ALU.mult, ALU.add).then_inc(halves_made, 1)
            v.tensor_scalar(before[:, :], iota_c[:, :], iota_p[:, 0:1], None, ALU.is_gt)
            v.tensor_scalar(ident[:, :], iota_c[:, :], iota_p[:, 0:1], None, ALU.is_equal)
            v.tensor_scalar(identb[:, :], iota_c[:, :], iota_p[:, 0:1], None, ALU.is_equal)
            v.tensor_copy(iota_cb[:, :], iota_c[:, :]).then_inc(consts, 1)

            dve.wait_ge(edges_in, 16 * 5)
            link(v.tensor_scalar(hi_i[:, :], edge_i["dst"][:, :], 7, None, ALU.arith_shift_right))
            v.tensor_copy(hi["dst"][:, :], hi_i[:, :]).then_inc(hi_made, 1)
            dve.wait_ge(hi_made, 1)
            link(v.tensor_scalar(hi_i[:, :], edge_i["src"][:, :], 7, None, ALU.arith_shift_right))
            link(v.tensor_copy(hi["src"][:, :], hi_i[:, :]))
            link(v.tensor_tensor(mask[:, 0:EC - 1], hi["dst"][:, 0:EC - 1], hi["dst"][:, 1:EC], ALU.is_gt))
            link(v.tensor_reduce(falls[:, 0:1], mask[:, 0:EC - 1], mybir.AxisListType.X, ALU.add))
            link(v.tensor_scalar(nexthi[0:EP - 1, :], nexthi[0:EP - 1, :], 7, None, ALU.arith_shift_right))
            link(v.tensor_copy(nexthif[0:EP - 1, :], nexthi[0:EP - 1, :]))
            link(v.tensor_tensor(falls[0:EP - 1, 1:2], hi["dst"][0:EP - 1, EC - 1:EC], nexthif[0:EP - 1, :], ALU.is_gt))
            link(v.tensor_tensor(fall[:, :], falls[:, 0:1], falls[:, 1:2], ALU.add))
            with dve.Fori(0, NW // HR) as i:
                steps.turn(i, 1, 0)
                for t in range(HR):
                    last = v.tensor_scalar(unread[t], hi["src"][:, :], iota_c[0:EP, ds(i * HR + t, 1)], 0.0,
                                           ALU.is_equal, ALU.add, accum_out=cnt["src"][:, ds(i * HR + t, 1)])
                link(last)
            steps.end(NW // HR)
            dve.wait_ge(x_in, 32)
            with dve.Fori(0, NW // HR) as i:
                steps.turn(i, 1, 0)
                for t in range(HR):
                    last = v.bn_stats(stats[:, ds(i * HR + t, 1), :].rearrange("p o s -> p (o s)"),
                                      xs[:, ds(i * HR + t, 1), :].rearrange("p o d -> p (o d)"))
                link(last)
            steps.end(NW // HR)
            v.tensor_copy(rec[:, :, F_DST], edge_i["dst"][:, :])
            v.tensor_copy(rec[:, :, F_SRC], edge_i["src"][:, :])
            v.tensor_copy(rec[:, :, F_TYPE], edge_i["t100"][:, :])
            v.scalar_tensor_tensor(rec[:, :, F_MSG].bitcast(I32), edge_i["src"][:, :], float(R8), edge_i["t8"][:, :],
                                   ALU.mult, ALU.add).then_inc(recs_made, 1)
            dve.wait_ge(signs_made, NW // HR)
            link(v.tensor_tensor(cnt["dst"][:, :], signs[:, 0:NW], signs[:, 1:NW + 1], ALU.subtract))
            v.tensor_scalar(cnt["dst"][:, :], cnt["dst"][:, :], 0.5, None, ALU.mult).then_inc(counted, 1)
            dve.wait_ge(totals, 1)
            for n, k in enumerate(("dst", "src")):
                link(v.tensor_copy(tot[k][:, :], bank[n][:, 0:NW]))
                link(v.tensor_tensor_scan(upto[k][:, :], tot[k][:, :], tot[k][:, :], 0.0, ALU.add, ALU.bypass))
                link(v.tensor_tensor(junkw[:, :], upto[k][:, :], tot[k][:, :], ALU.subtract))
                link(v.tensor_tensor(base[k][:, :], bank[n][0:EP, 64:64 + NW], junkw[0:EP, :], ALU.add))
            v.tensor_scalar(unsorted_i[:, :], bank[0][0:1, 128:129], 1.0, None, ALU.min).then_inc(flag_i, 1)
            for n, (s, k, size, kk, off) in enumerate((("d", "dst", P, KD, 0), ("s", "src", P * QB, KS, KD))):
                if n:
                    dve.wait_ge(table_out, 32)
                link(v.tensor_scalar(nblk_i[:, :], tot[k][:, :], float(size - 1), None, ALU.add))
                link(v.tensor_scalar(nblk_i[:, :], nblk_i[:, :], size.bit_length() - 1, None, ALU.arith_shift_right))
                link(v.tensor_copy(nblk[:, :], nblk_i[:, :]))
                link(v.tensor_tensor_scan(cumblk[:, :], nblk[:, :], nblk[:, :], 0.0, ALU.add, ALU.bypass))
                link(v.scalar_tensor_tensor(padded[:, :], nblk[:, :], float(size), tot[k][:, :], ALU.mult, ALU.subtract))
                for c in range(kk):
                    number = chunk_no[:, off + c:off + c + 1]
                    link(v.tensor_scalar(junkw[:, :], cumblk[:, :], number, 0.0, ALU.is_le, ALU.add,
                                         accum_out=wcol[:, c:c + 1]))
                    link(v.scalar_tensor_tensor(junkw[:, :], cumblk[:, :], number, padded[:, :], ALU.is_le, ALU.mult,
                                                accum_out=ocol[:, c:c + 1]))
                link(v.scalar_tensor_tensor(ocol[:, 0:kk], chunk_no[:, off:off + kk], float(size), ocol[:, 0:kk],
                                            ALU.mult, ALU.subtract))
                link(v.tensor_scalar(wcol[:, 0:kk], wcol[:, 0:kk], float(NW - 1), None, ALU.min))
                v.tensor_scalar(w128[:, 0:kk], wcol[:, 0:kk], float(P), None, ALU.mult)
                v.tensor_copy(wo_i[:, 1, 0:kk], wcol[:, 0:kk])
                v.tensor_scalar(wo_i[:, 0, 0:kk], ocol[:, 0:kk], float(E), None, ALU.min).then_inc(table_made, 1)

            dve.wait_ge(theta_done, 1)
            link(v.tensor_scalar(th[:, :], bank[3][:, 0:R], b2_sb[:, 0:1], None, ALU.add))
            link(v.tensor_scalar(whole[:, :], th[:, :], 0.15915494309189535, 0.25, ALU.mult, ALU.add))
            link(v.tensor_scalar(whole[:, :], whole[:, :], ROUND, None, ALU.add))
            link(v.tensor_scalar(whole[:, :], whole[:, :], ROUND, None, ALU.subtract))
            for part_of in (TWO_PI_A, TWO_PI_B, TWO_PI_C):
                link(v.scalar_tensor_tensor(th[:, :], whole[:, :], -part_of, th[:, :], ALU.mult, ALU.add))
            link(v.tensor_scalar(th[:, :], th[:, :], 1.5707963267948966, PI, ALU.add, ALU.min))
            v.tensor_scalar(th[:, :], th[:, :], -PI, None, ALU.max).then_inc(angle, 1)
            v.tensor_copy(rhs1[:, 0:D], wsb[:, 0, :])
            v.tensor_copy(rhs1[:, 128:129], wa[:, 1:2])
            v.tensor_copy(crow[:, 128:129], bank[3][0:1, 128:129])
            dve.wait_ge(cosine, 1)
            v.tensor_scalar(rhs1[:, T_S:TC], whole[:, :], wa[:, 2:3], wa[:, 0:1], ALU.mult, ALU.add).then_inc(rhs_ready, 1)

            def norm(n):
                even_m, even_v, odd_m, odd_v = (stats[:, :, c] for c in (1, 2, 4, 5))
                link(v.tensor_tensor(ln_d[:, :], even_m, odd_m, ALU.subtract))
                link(v.tensor_tensor(ln_m[:, :], even_m, odd_m, ALU.add))
                link(v.tensor_tensor(ln_v[:, :], even_v, odd_v, ALU.add))
                link(v.scalar_tensor_tensor(ln_d[:, :], ln_d[:, :], 0.25, ln_d[:, :], ALU.mult, ALU.mult))
                link(v.scalar_tensor_tensor(ln_v[:, :], ln_v[:, :], 1.0 / D, ln_d[:, :], ALU.mult, ALU.add))
                v.tensor_scalar(ln_v[:, :], ln_v[:, :], 1e-5, None, ALU.add).then_inc(var_ready, 1)
                dve.wait_ge(std_ready, n)
                link(v.reciprocal(ln_r[:, :], ln_d[:, :]))
                v.scalar_tensor_tensor(ln_b[:, :], ln_m[:, :], -0.5, ln_r[:, :], ALU.mult, ALU.mult).then_inc(ln_ready, 1)

            norm(1)
            @turns(dve, NW // HR)
            def _(i):
                def mark(t):
                    return steps.put(v.tensor_scalar(mask[:, :], hi["src"][:, :], iota_c[0:EP, ds(i * HR + t, 1)], None,
                                                     ALU.is_equal))

                def scan(t, marked):
                    steps.after(marked)
                    return steps.put(v.tensor_tensor_scan(rank[:, :], mask[:, :], mask[:, :],
                                                          base["src"][:, ds(i * HR + t, 1)], ALU.add, ALU.max))

                def pick(t, scanned):
                    since(dve, part_added, i * HR + max(t - 1, 0))
                    steps.after(scanned)
                    v.tensor_tensor(part[t % 2][:, :], mask[:, :], rank[:, :], ALU.mult).then_inc(part_made, 1)

                def middle(t):
                    dve.wait_ge(high, i * HR + t + 1)
                    since(dve, low, i * HR + t + 1 - HR)
                    v.tensor_tensor(rest[:, t, 0:TC], bank[2 + t % 4][:, 0:TC], part_of_table(i * HR + t, 0),
                                    ALU.subtract).then_inc(rest_mid, 1)

                steps.turn(i, 2 * HR)
                for t in range(HR + 1):
                    if t < HR:
                        since(dve, part_made, i * HR + t)
                        marked = mark(t)
                    if 1 <= t <= HR:
                        middle(t - 1)
                    if t < HR:
                        scanned = scan(t, marked)
                    if t < HR:
                        pick(t, scanned)
            steps.end(NW // HR)

            dve.wait_ge(flag_i, 1)
            unsorted = nc.values_load(unsorted_i[0:1, 0:1], engines=[ENG.DVE], min_val=0, max_val=1,
                                      skip_runtime_bounds_check_because="the flag is clamped to 0..1")
            with dve.If(unsorted):
                v.memset(pos["dst"][:, :], -1.0).then_inc(posd_cleared, 1)
                dve.wait_ge(posd_cleared, 1)
                with dve.Fori(0, NW) as b:
                    for t, make in enumerate((
                            lambda: v.tensor_scalar(mask[:, :], hi["dst"][:, :], iota_c[0:EP, ds(b, 1)], None, ALU.is_equal),
                            lambda: v.tensor_tensor_scan(rank[:, :], mask[:, :], mask[:, :], base["dst"][:, ds(b, 1)],
                                                         ALU.add, ALU.max),
                            lambda: v.tensor_tensor(part[0][:, :], mask[:, :], rank[:, :], ALU.mult),
                            lambda: v.tensor_tensor(pos["dst"][:, :], pos["dst"][:, :], part[0][:, :], ALU.add))):
                        make().then_inc(posd_step, 1)
                        dve.wait_ge(posd_step, 4 * b + t + 1)
                v.tensor_copy(pos_i[:, :], pos["dst"][:, :]).then_inc(posd_made, 1)

            dve.wait_ge(tables, 64)
            @turns(dve, TURNS_A)
            def _(i):
                steps.turn(i, 3 * HB)
                for k in range(HB):
                    p, n = k % 2, 2 * i + k // 2
                    dve.wait_ge(a_rec[k], 16 * GA * (i + 1))
                    link(v.tensor_tensor(rel_a[:, p, :], rec_a[:, k, :, F_DST],
                                         tab_w["d"][:, ds((i * HB + k) * GA, GA)], ALU.subtract))
                    since(dve, a_turned[p], n)
                    for j in range(GA):
                        last = v.tensor_scalar(one_a[:, p, j, :], iota_cb[:, :], rel_a[:, p, j:j + 1], None, ALU.is_equal)
                    last.then_inc(a_one[p], 1)
                    link(v.scalar_tensor_tensor(q_a[:, p, :], rel_a[:, p, :], -127.0, rel_a[:, p, :], ALU.add, ALU.mult))
                    link(v.tensor_scalar(m_a[:, p, :], q_a[:, p, :], 0.0, OUT, ALU.is_gt, ALU.mult))
                    since(dve, a_sent[k], 16 * GA * i)
                    v.tensor_copy(rows_a[:, k, :, C_SRC:ROW], rec_a[:, k, :, F_SRC:F_TYPE + 1])
                    v.tensor_tensor(idx_a[:, k, :], m_a[:, p, :], rec_a[:, k, :, F_POS], ALU.add).then_inc(a_idx[k], 1)
            steps.end(TURNS_A)

            def one_hot(i, k, windows):
                p, n = k % 2, HS // 2 * i + k // 2
                dve.wait_ge(b_rows[k], 16 * GB * (i + 1))
                link(v.tensor_tensor(rel_b[:, p, :, :], rows_b[:, k, :, :, C_SRC],
                                     windows.unsqueeze(2).to_broadcast([P, GB, QB]), ALU.subtract))
                since(dve, b_onew[k], i)
                v.tensor_tensor(one_a[:, k, :, :], iota_cb[:, :].unsqueeze(1).to_broadcast([P, CB, P]),
                                rel_b[:, p, :, :].rearrange("p b q -> p (b q)").unsqueeze(2).to_broadcast([P, CB, P]),
                                ALU.is_equal).then_inc(b_one[p], 1)

            def score(i, k):
                p, n = k % 2, HS // 2 * i + k // 2
                dve.wait_ge(b_got[p], n + 1)
                since(dve, b_wg[p], n)
                for s in range(CB):
                    last = v.scalar_tensor_tensor(junk_b[:, s, :], iota_c[:, 0:R], rows_b[:, k, s // QB, s % QB, C_TYPE:ROW],
                                                  bank[2 + 2 * p + s // 4][:, (s % 4) * R:(s % 4 + 1) * R],
                                                  ALU.is_equal, ALU.mult, accum_out=sel_b[:, p, s:s + 1])
                link(last)
                link(v.tensor_tensor(sc_b[:, p, :], sel_b[:, p, :],
                                     rows_b[:, k, :, :, C_A3].rearrange("p b q -> p (b q)"), ALU.add))
                v.scalar_tensor_tensor(lr_b[:, p, :], sc_b[:, p, :], 0.2, sc_b[:, p, :], ALU.mult, ALU.max).then_inc(b_lr[p], 1)

            one_hot(0, 0, tab_w["s"][:, 0:GB])

            @turns(dve, TURNS_B)
            def _(i):
                steps.turn(i, 1 + HS * 3)
                link(v.tensor_copy(near_b[:, :], tab_w["s"][:, ds((i * HS + 1) * GB, HS * GB)]))
                for k in range(HS):
                    one_hot(i + (k + 1) // HS, (k + 1) % HS, near_b[:, k * GB:(k + 1) * GB])
                    score(i, k)
            steps.end(TURNS_B)
            dve.wait_ge(b_added[1], HS // 2 * TURNS_B)

            link(v.tensor_scalar(ln_d[:, :], acc[:, :, C_ONE], 0.0, 1e-12, ALU.is_equal, ALU.mult))
            link(v.tensor_tensor(ln_d[:, :], ln_d[:, :], acc[:, :, C_ONE], ALU.add))
            link(v.reciprocal(rinv[:, :], ln_d[:, :]))
            def divide(i):
                w = ds(i * HR, HR)
                link(v.tensor_tensor(acc[:, w, 0:D], acc[:, w, 0:D],
                                     rinv[:, w].unsqueeze(2).to_broadcast([P, HR, D]), ALU.mult))
                v.sem_inc(z_ready, 1)

            def end_layer(i, last=False):
                steps.turn(i, 5)
                w = ds(i * HR, HR)
                since(dve, x_kept, i)
                link(v.scalar_tensor_tensor(xn[:, :, :], acc[:, w, 0:D], 0.0, xs[:, w, :], ALU.max, ALU.add))
                if not last:
                    divide(i + 1)
                dve.wait_ge(z_exp, i + 1)
                link(v.scalar_tensor_tensor(xn[:, :, :], ez[:, :, :], -1.0, xn[:, :, :], ALU.add, ALU.add))
                v.sem_inc(x_new, 1)
                for t in range(HR):
                    bn = v.bn_stats(xn_stats[:, t, :], xn[:, t, :])
                link(bn)
                link(v.tensor_copy(stats[:, w, :], xn_stats[:, :, :]))
            divide(0)
            turns(dve, NW // HR - 1)(end_layer)
            steps.end(NW // HR - 1)
            end_layer(NW // HR - 1, True)
            norm(2)
            @turns(dve, NW // HR)
            def _(i):
                for t in range(HR + 1):
                    if t < HR:
                        dve.wait_ge(h_turned, NW + i * HR + t + 1)
                        v.tensor_copy(hT[:, t, :], bank[t % 2][:, 0:P]).then_inc(hT_ready, 1)
                    if t >= 1:
                        dve.wait_ge(msg_done, i * HR + t)
                        since(dve, msg_out[t - 1], 16 * i)
                        for c in range(2):
                            last = v.tensor_tensor(
                                msg_o[:, t - 1, c * 512:(c + 1) * 512].rearrange("p (r d) -> p r d", d=D),
                                bank[2 + 2 * ((t - 1) % 3) + c][:, :].rearrange("p (r d) -> p r d", d=D),
                                bias_sb[:, :].unsqueeze(1).to_broadcast([P, 4, D]), ALU.add)
                        last.then_inc(msg_sum, 1)

            @turns(dve, TURNS_C)
            def _(i):
                steps.turn(i, HC * (1 + GC))
                for g in range(HC):
                    dve.wait_ge(c_rec[g], 16 * GC * (i + 1))
                    link(v.tensor_tensor(rel_c[:, g, :], rec_c[:, g, :, F_DST],
                                         tab_w["d"][:, ds(i * (GC * HC) + g * GC, GC)], ALU.subtract))
                    since(dve, c_sum[g], i)
                    for j in range(GC):
                        last = v.tensor_scalar(one_c[:, g, j, :], iota_c[:, :], rel_c[:, g, j:j + 1], None, ALU.is_equal)
                    last.then_inc(c_one[g], 1)
                for g in range(HC):
                    w = entries(ENG.DVE, "d", 1, i * (GC * HC) + g * GC, GC, NW - 1)
                    dve.wait_ge(c_sum[g], i + 1)
                    for j in range(GC):
                        here = xs[:, ds(w[j], 1), :].rearrange("p o d -> p (o d)")
                        link(v.tensor_tensor(here, here, bank[g][:, j * D:(j + 1) * D], ALU.add))
                    v.sem_inc(c_added[g], 1)
            steps.end(TURNS_C)
            v.sem_inc(x_done, 1)

        @block.scalar
        def _(act):
            s = nc.scalar
            act.wait_ge(halves_made, 1)
            act.wait_ge(hi_made, 1)

            def count_signs(i):
                since(act, signs_made, i)
                for t in range(HR):
                    last = s.activation(signs_out[:, t, :], hi["dst"][:, :], ACT.Sign, bias=halves[:, ds(i * HR + t, 1)],
                                        accum_out=signs[:, ds(i * HR + t, 1)])
                last.then_inc(signs_made, 1)

            count_signs(0)
            act.wait_ge(weightsT, 1)
            s.copy(wT[:, :], bank[4][:, 0:2 * P + R]).then_inc(wT_copied, 1)
            act.wait_ge(hid_done, 1)
            for k in range(HK):
                s.activation(hidT[:, k, :], bank[5][:, k * R:(k + 1) * R], ACT.Relu, bias=b1_sb[:, k:k + 1])
            s.copy(wa[:, :], bank[6][:, 0:3]).then_inc(hid_copied, 1)
            with act.Fori(1, NW // HR) as i:
                count_signs(i)

            act.wait_ge(angle, 1)
            s.activation(whole[:, :], th[:, :], ACT.Sin).then_inc(cosine, 1)

            def norm_turn(n, t, i):
                since(act, h_turned, (n - 1) * NW + i * HR + t + 1 - HR)
                w = i * HR + t
                s.activation(h_t[:, t, :], xs[:, ds(w, 1), :].rearrange("p o d -> p (o d)"), ACT.Relu,
                             bias=ln_b[:, ds(w, 1)], scale=ln_r[:, ds(w, 1)]).then_inc(h_ready, 1)

            act.wait_ge(var_ready, 1)
            s.activation(ln_d[:, :], ln_v[:, :], ACT.Sqrt).then_inc(std_ready, 1)
            act.wait_ge(ln_ready, 1)
            act.wait_ge(tails_out, 32)
            @turns(act, NW // HR)
            def _(i):
                for t in range(HR):
                    norm_turn(1, t, i)
                for t in range(HR + 2):
                    if t < HR:
                        act.wait_ge(h_turned, i * HR + t + 1)
                        s.copy(hT[:, t, :], bank[t % 2][:, 0:P]).then_inc(hT_ready, 1)
                    if 1 <= t <= HR:
                        act.wait_ge(dense, i * HR + t)
                        s.copy(part_of_table(i * HR + t - 1, 0), bank[2 + (t - 1) % 4][:, 0:TC]).then_inc(high, 1)
                    if t >= 2:
                        act.wait_ge(rest_mid, i * HR + t - 1)
                        s.copy(part_of_table(i * HR + t - 2, 1), rest[:, t - 2, 0:TC]).then_inc(mid, 1)

            act.wait_ge(low, NW)
            def copy_turned(turned, got, ready, p, n, chunks):
                act.wait_ge(turned[p], n + 1)
                since(act, got[p], n)
                s.copy(oneT_a[:, p, 0:chunks, :].rearrange("p j e -> p (j e)"),
                       bank[p][:, :].bitcast(BF16)[:, 0:chunks * P]).then_inc(ready[p], 1)

            @turns(act, TURNS_A)
            def _(i):
                for pair in range(0, HB, 2):
                    for k in (pair, pair + 1):
                        copy_turned(a_turned, a_got, a_oneT, k % 2, 2 * i + k // 2, GA)
                    for k in (pair, pair + 1):
                        p, n = k % 2, 2 * i + k // 2
                        act.wait_ge(a_got[p], n + 1)
                        since(act, a_sent[k], 16 * GA * i)
                        for b in range(2):
                            last = s.copy(rows_a[:, k, 2 * b:2 * b + 2, 0:T_S],
                                          bank[2 + 2 * p + b][:, 0:2 * T_S].rearrange("p (j c) -> p j c", j=2))
                        last.then_inc(a_rows[k], 1)

            copy_turned(b_turned, b_got, b_oneT, 0, 0, CB)

            def sums_out(i, k):
                p, n = k % 2, HS // 2 * i + k // 2
                act.wait_ge(b_sum[k], i + 1)
                since(act, b_added[p], n)
                s.copy(sums_b[:, p, :], bank[6 + p][:, 0:GB * ACC]).then_inc(b_out[p], 1)

            @turns(act, TURNS_B)
            def _(i):
                for k in range(HS):
                    if k >= 3:
                        sums_out(i, k - 3)
                    elif not isinstance(i, int):
                        sums_out(i - 1, k + HS - 3)
                    copy_turned(b_turned, b_got, b_oneT, (k + 1) % 2, HS // 2 * i + (k + 1) // 2, CB)
                    p, n = k % 2, HS // 2 * i + k // 2
                    act.wait_ge(b_lr[p], n + 1)
                    since(act, b_cap[p], n)
                    s.activation(wg_b[:, p, :], lr_b[:, p, :], ACT.Exp, scale=-1.0).then_inc(b_wg[p], 1)
            for k in range(HS - 3, HS):
                sums_out(TURNS_B - 1, k)

            @turns(act, NW // HR)
            def _(i):
                act.wait_ge(z_ready, i + 1)
                since(act, x_new, i)
                s.activation(ez[:, :, :], acc[:, ds(i * HR, HR), 0:D], ACT.Relu, scale=-1.0).then_inc(z_down, 1)
                act.wait_ge(z_down, i + 1)
                s.activation(ez[:, :, :], ez[:, :, :], ACT.Exp, scale=-1.0).then_inc(z_exp, 1)
                act.wait_ge(x_new, i + 1)
                s.copy(xs[:, ds(i * HR, HR), :], xn[:, :, :]).then_inc(x_kept, 1)
            act.wait_ge(var_ready, 2)
            s.activation(ln_d[:, :], ln_v[:, :], ACT.Sqrt).then_inc(std_ready, 1)
            act.wait_ge(ln_ready, 2)
            for t in range(HR):
                norm_turn(2, t, 0)

            def messages(i, last=False):
                for t in range(HR):
                    act.wait_ge(msg_sum, i * HR + t + 1)
                    s.activation(msg_o[:, t, :], msg_o[:, t, :], ACT.Relu).then_inc(msg_ready, 1)
                    if not last:
                        norm_turn(2, t, i + 1)
            turns(act, NW // HR - 1)(messages)
            messages(NW // HR - 1, True)

        @block.tensor
        def _(pe):
            t_ = nc.tensor

            def mm(o, l, r, start=True, stop=True):
                return t_.matmul(o, l, r, start=start, stop=stop)

            pe.wait_ge(consts, 2)
            pe.wait_ge(weights_in, 16 * 11)
            t_.transpose(bank[4][:, 0:P], wsb[:, 0, :], ident[:, :])
            t_.transpose(bank[4][:, P:2 * P], wsb[:, 1, :], ident[:, :])
            t_.transpose(bank[4][:, 2 * P:2 * P + R], emb_sb[:, :], ident[0:R, 0:R]).then_inc(weightsT, 1)
            pe.wait_ge(wT_copied, 1)
            embT = wT[:, 2 * P:2 * P + R]
            for k in range(HK):
                mm(bank[5][:, k * R:(k + 1) * R], w1_sb[:, k * P:(k + 1) * P], embT)
            mm(bank[6][:, 0:1], wT[:, 0:P], a_sb[:, 0:1])
            mm(bank[6][:, 1:2], wT[:, 0:P], a_sb[:, 2:3])
            mm(bank[6][:, 2:3], wT[:, P:2 * P], a_sb[:, 1:2]).then_inc(hid_done, 1)
            pe.wait_ge(hid_copied, 1)
            for k in range(HK):
                mm(bank[3][:, 0:R], w2_sb[:, k, :], hidT[:, k, :], k == 0, k == HK - 1)
            mm(bank[3][0:1, 128:129], cr_sb[:, :], wa[:, 2:3]).then_inc(theta_done, 1)
            pe.wait_ge(counted, 1)
            for n, k in enumerate(("dst", "src")):
                mm(bank[n][:, 0:NW], ones[0:EP, :], cnt[k][:, :])
                mm(bank[n][0:EP, 64:64 + NW], before[0:EP, 0:EP], cnt[k][:, :])
            mm(bank[0][0:1, 128:129], fall[:, :], ones[0:EP, 0:1]).then_inc(totals, 1)

            pe.wait_ge(rhs_ready, 1)
            pe.wait_ge(flag_i, 1)
            def turn_features(n, i, t):
                done = (n - 1) * NW + i * HR
                pe.wait_ge(h_ready, done + t + 1)
                since(pe, hT_ready, done + max(t - 1, 0))
                t_.transpose(bank[t % 2][:, 0:P], h_t[:, t, :], ident[:, :]).then_inc(h_turned, 1)

            @turns(pe, NW // HR)
            def _(i):
                for t in range(HR + 1):
                    if t < HR:
                        turn_features(1, i, t)
                    if t >= 1:
                        pe.wait_ge(hT_ready, i * HR + t)
                        since(pe, rest_mid, i * HR + max(t - 4, 0))
                        to = bank[2 + (t - 1) % 4][:, 0:TC]
                        mm(to, hT[:, t - 1, :], rhs1[:, 0:TC], True, False)
                        mm(to, ones[0:1, :], crow[:, 0:TC], False, True).then_inc(dense, 1)

            pe.wait_ge(low, NW)
            pe.wait_ge(tables, 64)
            def turn_one_hot(one, ready, turned, slot, p, n, chunks):
                pe.wait_ge(one[p], n + 1)
                since(pe, ready[p], n)
                for j in range(chunks):
                    last = t_.transpose(bank[p][:, :].bitcast(BF16)[:, j * P:(j + 1) * P], one_a[:, slot, j, :], identb[:, :])
                last.then_inc(turned[p], 1)

            @turns(pe, TURNS_A)
            def _(i):
                for pair in range(0, HB, 2):
                    for k in (pair, pair + 1):
                        turn_one_hot(a_one, a_oneT, a_turned, k % 2, k % 2, 2 * i + k // 2, GA)
                    for k in (pair, pair + 1):
                        p, n = k % 2, 2 * i + k // 2
                        w = entries(ENG.PE, "d", 1, (i * HB + k) * GA, GA, NW - 1)
                        pe.wait_ge(a_oneT[p], n + 1)
                        slot, used = before2(k, i)
                        since(pe, a_rows[slot], used)
                        for j in range(GA):
                            to = bank[2 + 2 * p + j // 2][:, (j % 2) * T_S:(j % 2 + 1) * T_S]
                            for c in range(3):
                                last = mm(to, oneT_a[:, p, j, :], table[:, ds(w[j], 1), c, 0:T_S].rearrange(
                                    "p o c -> p (o c)"), c == 0, c == 2)
                        last.then_inc(a_got[p], 1)

            def src_scores(i, k):
                p, n = k % 2, HS // 2 * i + k // 2
                w = entries(ENG.PE, "s", 1, (i * HS + k) * GB, GB, NW - 1)
                pe.wait_ge(b_oneT[p], n + 1)
                since(pe, b_lr[p], n)
                for j in range(CB):
                    to = bank[2 + 2 * p + j // 4][:, (j % 4) * R:(j % 4 + 1) * R]
                    for c in range(3):
                        last = mm(to, oneT_a[:, p, j, :],
                                  table[:, ds(w[j // QB], 1), c, T_S:TC].rearrange("p o c -> p (o c)"), c == 0, c == 2)
                last.then_inc(b_got[p], 1)

            def weighted_sums(i, k):
                p, n = k % 2, HS // 2 * i + k // 2
                pe.wait_ge(b_onew[k], i + 1)
                since(pe, b_out[p], n)
                for b in range(GB):
                    for q in range(QB):
                        last = mm(bank[6 + p][:, b * ACC:(b + 1) * ACC], onew_b[:, p, b * QB + q, :],
                                  rows_b[:, k, b, q, 0:ACC], q == 0, q == QB - 1)
                last.then_inc(b_sum[k], 1)

            turn_one_hot(b_one, b_oneT, b_turned, 0, 0, 0, CB)

            @turns(pe, TURNS_B)
            def _(i):
                for k in range(HS):
                    src_scores(i, k)
                    turn_one_hot(b_one, b_oneT, b_turned, (k + 1) % HS, (k + 1) % 2, HS // 2 * i + (k + 1) // 2, CB)
                    if k >= 2:
                        weighted_sums(i, k - 2)
                    elif not isinstance(i, int):
                        weighted_sums(i - 1, k + HS - 2)
            for k in (HS - 2, HS - 1):
                weighted_sums(TURNS_B - 1, k)

            w8v = w8_sb[:, :, :].rearrange("p r n -> p (r n)")
            @turns(pe, NW // HR)
            def _(i):
                for t in range(HR + 1):
                    if t < HR:
                        turn_features(2, i, t)
                    if t >= 1:
                        pe.wait_ge(hT_ready, NW + i * HR + t)
                        since(pe, msg_sum, i * HR + max(t - 3, 0))
                        for c in range(2):
                            last = mm(bank[2 + 2 * ((t - 1) % 3) + c][:, :], hT[:, t - 1, :], w8v[:, c * 512:(c + 1) * 512])
                        last.then_inc(msg_done, 1)

            pe.wait_ge(msg_sum, NW)
            @turns(pe, TURNS_C)
            def _(i):
                for g in range(HC):
                    pe.wait_ge(c_one[g], i + 1)
                    pe.wait_ge(c_msg[g], 16 * GC * (i + 1))
                    since(pe, c_added[g], i)
                    for j in range(GC):
                        last = mm(bank[g][:, j * D:(j + 1) * D], one_c[:, g, j, :], msg_c[:, g, j, :])
                    last.then_inc(c_sum[g], 1)


_INS = ['x', 'src', 'dst', 'edge_type_100', 'edge_type_8', 'L0_gnn_relation_embeds', 'L0_gnn_mlp_w1', 'L0_gnn_mlp_b1',
        'L0_gnn_mlp_w2', 'L0_gnn_mlp_b2', 'L0_gnn_c_r', 'L0_gnn_W', 'L0_gnn_W_r', 'L0_gnn_a', 'L1_gnn_weight',
        'L1_gnn_bias']


def kernel(**inputs):
    import numpy as _np
    import concourse.bacc as _bacc
    from concourse import mybir as _mybir
    from concourse.bass_utils import run_bass_kernel_spmd as _run

    nc = _bacc.Bacc("TRN2", target_bir_lowering=False, num_devices=1)
    arrays, args = {}, []
    for name in _INS:
        a = _np.ascontiguousarray(inputs[name])
        arrays[f"in_{name}"] = a
        args.append(nc.dram_tensor(f"in_{name}", a.shape, _mybir.dt.from_np(a.dtype), kind="ExternalInput").ap())
    out = nc.dram_tensor("out_x", (N, D), F32, kind="ExternalOutput").ap()
    build(nc, *args, out)
    r = _run(nc, [arrays], core_ids=[0])
    return r.results[0]["out_x"]
```

```python
from contextlib import ExitStack

import concourse.bass as bass
from concourse import mybir

ALU = mybir.AluOpType
ACT = mybir.ActivationFunctionType
ENG = mybir.EngineType
F32 = mybir.dt.float32
BF16 = mybir.dt.bfloat16
I32 = mybir.dt.int32
ds = bass.ds

P = 128
N, D = 6250, 128
NW = -(-N // P)
LASTN = N - (NW - 1) * P
E = 100000
EP, EC = 125, 800
R = 100
HID = 512
HK = HID // P
R8 = 8

F_DST, F_POS, F_SRC, F_TYPE, F_MSG, NF = 0, 1, 2, 3, 4, 5
C_A3, C_ONE, C_SRC, C_TYPE, ROW = 128, 129, 130, 131, 132
ACC = 130
T_S, TC, TS = 129, 229, 230
FAR = 1.0e6
OUT = 1048576.0

HB, HS = 4, 6
GA = 4
TURNS_A = -(-(-(-E // P) + NW) // (HB * GA))
CHUNKS_D = TURNS_A * HB * GA
FIRST = 25
TURNS_FIRST = FIRST * EC // (P * HB * GA)
QB, GB = 4, 2
CB = QB * GB
GROUPS_B = -(-(-(-E // (P * QB)) + NW) // GB)
TURNS_B, REST_B = GROUPS_B // HS, GROUPS_B % HS
assert 3 <= REST_B <= HS - 2
BLOCKS_S = (GROUPS_B + 2) * GB
GC, HC = 4, 4
TURNS_C = CHUNKS_D // (GC * HC)
assert TURNS_C * GC * HC == CHUNKS_D
KD = -(-CHUNKS_D // P)
KS = -(-BLOCKS_S // P)
TAIL = P * QB

TWO_PI_A = 6.28125
TWO_PI_B = 0.0019350051879882812
TWO_PI_C = 6.283185307179586 - TWO_PI_A - TWO_PI_B
PI = 3.1415925
TOP = 3.4028234e38
ROUND = 12582912.0


def build(nc, x, src, dst, t100, t8, emb, w1, b1, w2, b2, c_r, W, W_r, a, w8, bias, out):
    with ExitStack() as ctx:
        def sb(name, shape, dt=F32):
            return ctx.enter_context(nc.sbuf_tensor(name, shape, dt))

        def sem(name):
            return ctx.enter_context(nc.semaphore(name))

        def dram(name, shape, dt=F32):
            return nc.dram_tensor(name, shape, dt, kind="Internal").ap()

        bank = [ctx.enter_context(nc.psum_tensor(f"bank{i}", [P, 512], F32)) for i in range(8)]

        rec_d = dram("rec_d", [E + TAIL, NF])
        rows_d = dram("rows_d", [E + TAIL, ROW])
        msg_d = dram("msg_d", [NW * P * R8, D])
        tabw_d = {s: dram(f"tabw_{s}", [P * k]) for s, k in (("d", KD), ("s", KS))}
        tabi_d = {s: dram(f"tabi_{s}", [2, P * k], I32) for s, k in (("d", KD), ("s", KS))}

        iota_c = sb("iota_c", [P, P])
        iota_p = sb("iota_p", [P, 1])
        iota_cb = sb("iota_cb", [P, P], BF16)
        ident = sb("ident", [P, P])
        identb = sb("identb", [P, P], BF16)
        before = sb("before", [P, P])
        ones = sb("ones", [P, P])
        farrec = sb("farrec", [P, QB * NF])
        chunk_no = sb("chunk_no", [P, KD + KS])

        area = sb("area", [P, NW * ACC + HS * CB * ROW + 2 * CB * P])
        assert NW * ACC + HS * CB * ROW + 2 * CB * P >= EC * (NF + 13)

        def column(n, dt=F32):
            view = area[0:EP, EC * (NF + n):EC * (NF + n + 1)]
            return view if dt == F32 else view.bitcast(dt)

        rec = area[0:EP, 0:EC * NF].rearrange("p (c f) -> p c f", f=NF)
        edge_i = {k: column(n, I32) for n, k in enumerate(("src", "dst", "t100", "t8"))}
        hi_i = column(4, I32)
        hi = {"src": column(5, BF16)[:, 0:EC], "dst": column(5, BF16)[:, EC:2 * EC]}
        mask = [column(6, BF16)[:, 0:EC], column(6, BF16)[:, EC:2 * EC]]
        rank = column(7)
        part = [column(8), column(9)]
        pos = {"src": column(10), "dst": column(11)}
        pos_i = column(12, I32)
        unread = [column(n, BF16)[:, f:f + EC] for n in (7, 8, 9, 12) for f in (0, EC)]
        nexthi = sb("nexthi", [EP, 1], I32)
        nexthif = sb("nexthif", [EP, 1])
        cnt = {k: sb(f"cnt_{k}", [EP, NW]) for k in ("src", "dst")}
        tot = {k: sb(f"tot_{k}", [P, NW]) for k in ("src", "dst")}
        upto = {k: sb(f"upto_{k}", [P, NW]) for k in ("src", "dst")}
        base = {k: sb(f"base_{k}", [EP, NW]) for k in ("src", "dst")}
        signs = sb("signs", [EP, NW + 1])
        halves = sb("halves", [EP, NW])
        nblk = sb("nblk", [P, NW])
        nblk_i = sb("nblk_i", [P, NW], I32)
        cumblk = sb("cumblk", [P, NW])
        padded = sb("padded", [P, NW])
        junkw = sb("junkw", [P, NW])
        wcol = sb("wcol", [P, KD])
        ocol = sb("ocol", [P, KD])
        w128 = sb("w128", [P, KD])
        wo_i = sb("wo_i", [P, 2, KD], I32)
        falls = sb("falls", [EP, 2])
        fall = sb("fall", [EP, 1])
        unsorted_i = sb("unsorted_i", [1, 1], I32)
        tab_i = {"d": sb("tab_i_d", [2, P * KD], I32), "s": sb("tab_i_s", [2, P * KS], I32)}
        tab_w = {"d": sb("tab_w_d", [P, P * KD]), "s": sb("tab_w_s", [P, P * KS])}
        idx_slot = sb("idx_slot", [EP, 1], I32)
        rec_slot = sb("rec_slot", [EP, NF])

        xs = sb("xs", [P, NW, D])
        stats = sb("stats", [P, NW, 6])
        ln_m = sb("ln_m", [P, NW])
        ln_v = sb("ln_v", [P, NW])
        ln_d = sb("ln_d", [P, NW])
        ln_r = sb("ln_r", [P, NW])
        ln_b = sb("ln_b", [P, NW])
        HR = 7
        MSG_BANKS = (0, 1, 2, 0, 1, 2, 1)
        h_t = sb("h_t", [P, HR, D])
        hT = sb("hT", [P, HR, P])
        rest = area[:, EC * (NF + 11):EC * (NF + 11) + HR * TS].rearrange("p (t c) -> p t c", t=HR)
        table = sb("table", [P, NW, 3, TS], BF16)
        table_flat = table[:, :, :, :].rearrange("p w k c -> p (w k c)")
        signs_out = table_flat[0:EP, 0:HR * EC].rearrange("p (t c) -> p t c", t=HR)
        far = table_flat[:, HR * EC:HR * EC + 2 * QB * ROW].bitcast(F32)
        acc = area[:, 0:NW * ACC].rearrange("p (w c) -> p w c", c=ACC)
        rinv = sb("rinv", [P, NW])
        ez = area[:, NW * ACC:NW * ACC + HR * D].rearrange("p (t c) -> p t c", t=HR)

        wsb = sb("wsb", [P, 2, P])
        emb_sb = sb("emb_sb", [R, D])
        onehots = sb("onehots", [P, HC * GC * P])
        w1_sb = onehots[:, 0:HID]
        w2_sb = onehots[:, HID:2 * HID].rearrange("p (k n) -> p k n", n=P)
        wT = onehots[:, 2 * HID:2 * HID + 2 * P + R]
        b1_sb = sb("b1_sb", [P, HK])
        b2_sb = sb("b2_sb", [P, 1])
        cr_sb = sb("cr_sb", [P, 1])
        a_sb = sb("a_sb", [P, 3])
        w8_sb = sb("w8_sb", [P, R8, P])
        bias_sb = sb("bias_sb", [P, P])
        wa = sb("wa", [P, 3])
        xn = area[:, NW * ACC + HR * D:NW * ACC + 2 * HR * D].rearrange("p (t c) -> p t c", t=HR)
        xn_stats = sb("xn_stats", [P, HR, 6])
        rhs1 = sb("rhs1", [P, TS])
        crow = sb("crow", [1, TS])

        rec_a = sb("rec_a", [P, HB, GA, NF])
        rel_a = sb("rel_a", [P, 2, GA])
        q_a = sb("q_a", [P, 2, GA])
        m_a = sb("m_a", [P, 2, GA])
        idx_a = sb("idx_a", [P, HB, GA], I32)
        one_a = sb("one_a", [P, HS, CB, P], BF16)
        early = one_a[:, :, :, :].rearrange("p h s e -> p (h s e)").bitcast(F32)
        hidT = early[:, 0:HK * R].rearrange("p (k r) -> p k r", k=HK)
        th = early[:, HK * R:(HK + 1) * R]
        whole = early[:, (HK + 1) * R:(HK + 2) * R]
        oneT_a = sb("oneT_a", [P, 2, CB, P], BF16)
        ring = NW * ACC
        rows_a = area[:, ring:ring + HB * GA * ROW].rearrange("p (h j f) -> p h j f", h=HB, j=GA)
        rows_b = area[:, ring:ring + HS * CB * ROW].rearrange("p (h b q f) -> p h b q f", h=HS, b=GB, q=QB)
        onew_b = area[:, ring + HS * CB * ROW:ring + HS * CB * ROW + 2 * CB * P].rearrange(
            "p (h s e) -> p h s e", h=2, s=CB)
        msg_c = area[:, ring:ring + HC * GC * D].rearrange("p (g j d) -> p g j d", g=HC, j=GC)
        near_b = sb("near_b", [P, HS * GB])
        rel_b = sb("rel_b", [P, 2, GB, QB])
        junk_b = onehots[:, 2 * GB * ACC:2 * GB * ACC + CB * R // 2].bitcast(BF16).rearrange("p (s r) -> p s r", s=CB)
        sel_b = sb("sel_b", [P, 2, CB])
        sc_b = sb("sc_b", [P, 2, CB])
        lr_b = sb("lr_b", [P, 2, CB])
        wg_b = sb("wg_b", [P, 2, CB])
        cap_b = sb("cap_b", [P, 2, CB])
        rec_c = sb("rec_c", [P, HC, GC, NF])
        rel_c = sb("rel_c", [P, HC, GC])
        sums_b = onehots[:, 0:2 * GB * ACC].rearrange("p (h c) -> p h c", h=2)
        one_c = onehots[:, :].rearrange("p (g j e) -> p g j e", g=HC, j=GC)
        msg_o = area[:, NW * ACC:NW * ACC + HR * R8 * D].rearrange("p (t c) -> p t c", t=HR)

        edges_in = sem("edges_in")
        weights_in = sem("weights_in")
        x_in = sem("x_in")
        iotas = sem("iotas")
        consts = sem("consts")
        vstep = sem("vstep")
        pstep = sem("pstep")
        counted = sem("counted")
        totals = sem("totals")
        flag_i = sem("flag_i")
        table_made = sem("table_made")
        table_out = sem("table_out")
        tables = sem("tables")
        recs_made = sem("recs_made")
        posd_made = sem("posd_made")
        posd_step = sem("posd_step")
        posd_cleared = sem("posd_cleared")
        signs_made = sem("signs_made")
        halves_made = sem("halves_made")
        hi_made = sem("hi_made")
        part_made = sem("part_made")
        part_added = sem("part_added")
        recs_out = sem("recs_out")
        first_out = sem("first_out")
        slot_out = sem("slot_out")
        tails_made = sem("tails_made")
        tails_out = sem("tails_out")
        weightsT = sem("weightsT")
        wT_copied = sem("wT_copied")
        hid_done = sem("hid_done")
        hid_copied = sem("hid_copied")
        theta_done = sem("theta_done")
        angle = sem("angle")
        cosine = sem("cosine")
        rhs_ready = sem("rhs_ready")
        var_ready = sem("var_ready")
        std_ready = sem("std_ready")
        ln_ready = sem("ln_ready")
        h_ready = sem("h_ready")
        h_turned = sem("h_turned")
        hT_ready = sem("hT_ready")
        dense = sem("dense")
        high = sem("high")
        rest_mid = sem("rest_mid")
        mid = sem("mid")
        low = sem("low")
        a_rec = [sem(f"a_rec{h}") for h in range(HB)]
        a_idx = [sem(f"a_idx{h}") for h in range(HB)]
        a_one = [sem(f"a_one{h}") for h in range(2)]
        a_turned = [sem(f"a_turned{h}") for h in range(2)]
        a_oneT = [sem(f"a_oneT{h}") for h in range(2)]
        a_got = [sem(f"a_got{h}") for h in range(2)]
        a_rows = [sem(f"a_rows{h}") for h in range(HB)]
        a_sent = [sem(f"a_sent{h}") for h in range(HB)]
        b_rows = [sem(f"b_rows{h}") for h in range(HS)]
        b_near = sem("b_near")
        b_rel = [sem(f"b_rel{h}") for h in range(2)]
        b_one = [sem(f"b_one{h}") for h in range(2)]
        b_turned = [sem(f"b_turned{h}") for h in range(2)]
        b_oneT = [sem(f"b_oneT{h}") for h in range(2)]
        b_got = [sem(f"b_got{h}") for h in range(2)]
        b_lr = [sem(f"b_lr{h}") for h in range(2)]
        b_cap = [sem(f"b_cap{h}") for h in range(2)]
        b_wg = [sem(f"b_wg{h}") for h in range(2)]
        held = sem("held")
        b_onew = [sem(f"b_onew{h}") for h in range(HS)]
        b_sum = [sem(f"b_sum{h}") for h in range(HS)]
        b_out = [sem(f"b_out{h}") for h in range(2)]
        b_half = sem("b_half")
        b_added = [sem(f"b_added{h}") for h in range(2)]
        rinv_made = sem("rinv_made")
        z_ready = sem("z_ready")
        z_exp = sem("z_exp")
        z_down = sem("z_down")
        x_new = sem("x_new")
        x_kept = sem("x_kept")
        msg_done = sem("msg_done")
        msg_sum = sem("msg_sum")
        msg_ready = sem("msg_ready")
        msg_out = [sem(f"msg_out{t}") for t in range(HR)]
        c_rec = [sem(f"c_rec{g}") for g in range(HC)]
        c_one = [sem(f"c_one{g}") for g in range(HC)]
        c_msg = [sem(f"c_msg{g}") for g in range(HC)]
        c_sum = [sem(f"c_sum{g}") for g in range(HC)]
        c_added = [sem(f"c_added{g}") for g in range(HC)]
        x_done = sem("x_done")
        out_done = sem("out_done")

        def entries(engine, side, which, first, count, top):
            _, values = nc.values_load_multi_w_load_instructions(
                tab_i[side][which:which + 1, ds(first, count)], engines=[engine], min_val=0, max_val=top,
                skip_runtime_bounds_check_because="the table is clamped to 0..top where it is made")
            return values

        def part_of_table(window, k):
            return table[:, ds(window, 1), k, 0:TC].rearrange("p o c -> p (o c)")

        def since(eng, s, value):
            if not isinstance(value, int) or value > 0:
                eng.wait_ge(s, value)

        def turns(eng, count):
            def run(body):
                body(0)
                with eng.Fori(1, count) as i:
                    body(i)
            return run

        class Chain:

            def __init__(self, eng, s):
                self.eng, self.s, self.n, self.k = eng, s, 0, 0

            def link(self, ins):
                ins.then_inc(self.s, 1)
                self.k += 1
                self.eng.wait_ge(self.s, self.n + self.k)

            def put(self, ins):
                ins.then_inc(self.s, 1)
                self.k += 1
                return self.n + self.k

            def after(self, value):
                self.eng.wait_ge(self.s, value)

            def turn(self, i, each, start=1):
                self.n, self.k = self.n + self.k, 0
                if not isinstance(i, int):
                    self.first, self.each, self.start = self.n, each, start
                    self.n = self.first + (i - start) * each

            def end(self, count):
                assert self.k == self.each, (self.k, self.each)
                self.n, self.k = self.first + (count - self.start) * self.each, 0

        def before2(k, i, slots=HB):
            return (k - 2, i + 1) if k >= 2 else (k - 2 + slots, i)

        block = ctx.enter_context(nc.Block())

        @block.sync
        def _(sp):
            for k, v in (("dst", dst), ("src", src), ("t100", t100), ("t8", t8)):
                sp.dma_start(edge_i[k][:, :], v.rearrange("(p c) -> p c", p=EP)).then_inc(edges_in, 16)
            with nc.allow_non_contiguous_dma(reason="one value of each partition's first edge"):
                sp.dma_start(nexthi[0:EP - 1, :], dst.rearrange("(p c) -> p c", p=EP)[1:EP, 0:1]).then_inc(edges_in, 16)
            sp.dma_start(wsb[:, 0, :], W).then_inc(weights_in, 16)
            sp.dma_start(wsb[:, 1, :], W_r).then_inc(weights_in, 16)
            sp.dma_start(emb_sb[:, :], emb).then_inc(weights_in, 16)
            sp.dma_start(w1_sb[:, :], w1).then_inc(weights_in, 16)
            sp.dma_start(w2_sb[:, :, :], w2.rearrange("(k p) n -> p k n", p=P)).then_inc(weights_in, 16)
            sp.dma_start(w8_sb[:, :, :], w8.rearrange("r p n -> p r n")).then_inc(weights_in, 16)
            with nc.allow_non_contiguous_dma(reason="short vectors turned onto the partitions"):
                sp.dma_start(b1_sb[:, :], b1.rearrange("(k p) -> p k", p=P)).then_inc(weights_in, 16)
                sp.dma_start(b2_sb[:, :], b2.rearrange("(p o) -> p o", o=1)).then_inc(weights_in, 16)
                sp.dma_start(cr_sb[:, :], c_r.rearrange("o p -> p o")).then_inc(weights_in, 16)
                sp.dma_start(a_sb[:, :], a.rearrange("(k p) -> p k", p=P)).then_inc(weights_in, 16)
            sp.dma_start(bias_sb[:, :], bias.rearrange("(o n) -> o n", o=1).to_broadcast([P, P])).then_inc(weights_in, 16)
            sp.dma_start(xs[:, 0:NW - 1, :], x[0:(NW - 1) * P, :].rearrange("(w p) d -> p w d", p=P)).then_inc(x_in, 16)
            sp.wait_ge(consts, 1)
            sp.dma_start(xs[0:LASTN, NW - 1, :], x[(NW - 1) * P:N, :]).then_inc(x_in, 16)
            sp.wait_ge(tails_made, 1)
            sp.dma_start(rows_d[E:E + TAIL, :].rearrange("(p q) f -> p (q f)", p=P), far[:, :]).then_inc(tails_out, 16)
            sp.dma_start(rec_d[E:E + TAIL, :].rearrange("(p q) f -> p (q f)", p=P), farrec[:, :]).then_inc(tails_out, 16)
            for n, (s, k) in enumerate((("d", KD), ("s", KS))):
                sp.wait_ge(table_made, n + 1)
                sp.dma_start(tabw_d[s].rearrange("(p k) -> p k", p=P), w128[:, 0:k]).then_inc(table_out, 16)
                sp.dma_start(tabi_d[s].rearrange("t (p k) -> p t k", p=P), wo_i[:, :, 0:k]).then_inc(table_out, 16)
                sp.wait_ge(table_out, 32 * (n + 1))
                sp.dma_start(tab_i[s][:, :], tabi_d[s]).then_inc(tables, 16)
                sp.dma_start(tab_w[s][:, :], tabw_d[s].rearrange("(o c) -> o c", o=1).to_broadcast([P, P * k])).then_inc(tables, 16)
            sp.wait_ge(tables, 64)
            sp.wait_ge(tails_out, 32)

            sp.wait_ge(recs_out, 1)
            def load_records(i):
                for k in range(HB):
                    since(sp, a_idx[k], i)
                    o = entries(ENG.SP, "d", 0, (i * HB + k) * GA, GA, E)
                    for j in range(GA):
                        sp.dma_start(rec_a[:, k, j, :], rec_d[ds(o[j], P), :]).then_inc(a_rec[k], 16)
            turns(sp, TURNS_FIRST)(load_records)
            sp.wait_ge(recs_out, 2)
            with sp.Fori(TURNS_FIRST, TURNS_A) as i:
                load_records(i)

            for k in range(HB):
                sp.wait_ge(a_sent[k], 16 * GA * TURNS_A)

            def load_rows(i, k):
                since(sp, b_sum[k], i)
                o = entries(ENG.SP, "s", 0, (i * HS + k) * GB, GB, E)
                for b in range(GB):
                    sp.dma_start(rows_b[:, k, b, :, :], rows_d[ds(o[b], P * QB), :].rearrange(
                        "(p q) f -> p q f", q=QB)).then_inc(b_rows[k], 16)

            @turns(sp, TURNS_B)
            def _(i):
                for k in range(HS):
                    load_rows(i, k)
            for k in range(REST_B + 2):
                load_rows(TURNS_B, k)

            msg_v = msg_d.rearrange("(w p r) d -> p w (r d)", p=P, r=R8)
            @turns(sp, NW // HR)
            def _(i):
                for t in range(HR):
                    sp.wait_ge(msg_ready, i * HR + t + 1)
                    sp.dma_start(msg_v[:, ds(i * HR + t, 1), :], msg_o[:, t:t + 1, :]).then_inc(msg_out[t], 16)

            @turns(sp, TURNS_C)
            def _(i):
                for g in range(HC):
                    since(sp, c_msg[g], 16 * GC * i)
                    since(sp, c_one[g], i)
                    o = entries(ENG.SP, "d", 0, i * (GC * HC) + g * GC, GC, E)
                    for j in range(GC):
                        sp.dma_start(rec_c[:, g, j, :], rec_d[ds(o[j], P), :]).then_inc(c_rec[g], 16)

            sp.wait_ge(x_done, 1)
            sp.dma_start(out[0:(NW - 1) * P, :].rearrange("(w p) d -> p w d", p=P), xs[:, 0:NW - 1, :]).then_inc(out_done, 16)
            sp.dma_start(out[(NW - 1) * P:N, :], xs[0:LASTN, NW - 1, :]).then_inc(out_done, 16)
            sp.wait_ge(out_done, 32)

        @block.gpsimd
        def _(pool):
            steps = Chain(pool, pstep)
            steps.link(nc.gpsimd.memset(pos["src"][:, :], -1.0))
            nc.gpsimd.iota(iota_c[:, :], pattern=[[1, P]], base=0, channel_multiplier=0,
                           allow_small_or_imprecise_dtypes=True).then_inc(iotas, 1)
            nc.gpsimd.iota(iota_p[:, :], pattern=[[0, 1]], base=0, channel_multiplier=1,
                           allow_small_or_imprecise_dtypes=True).then_inc(iotas, 1)
            nc.gpsimd.iota(chunk_no[:, 0:KD], pattern=[[1, KD]], base=0, channel_multiplier=KD,
                           allow_small_or_imprecise_dtypes=True).then_inc(iotas, 1)
            nc.gpsimd.iota(chunk_no[:, KD:KD + KS], pattern=[[1, KS]], base=0, channel_multiplier=KS,
                           allow_small_or_imprecise_dtypes=True).then_inc(iotas, 1)
            nc.gpsimd.memset(far[:, :], FAR)
            steps.link(nc.gpsimd.memset(farrec[:, :], FAR))
            nc.gpsimd.memset(farrec[:, :].rearrange("p (q f) -> p q f", f=NF)[:, :, F_MSG], 0.0).then_inc(tails_made, 1)

            with pool.Fori(0, NW // HR) as i:
                for t in range(HR):
                    pool.wait_ge(part_made, i * HR + t + 1)
                    nc.gpsimd.tensor_tensor(pos["src"][:, :], pos["src"][:, :], part[t % 2][:, :], ALU.add).then_inc(part_added, 1)
                    pool.wait_ge(mid, i * HR + t + 1)
                    nc.gpsimd.tensor_tensor(part_of_table(i * HR + t, 2), rest[:, t, 0:TC], part_of_table(i * HR + t, 1),
                                            ALU.subtract).then_inc(low, 1)
                    pool.wait_ge(part_added, i * HR + t + 1)

            pool.wait_ge(recs_made, 1)
            pool.wait_ge(flag_i, 1)
            unsorted = nc.values_load(unsorted_i[0:1, 0:1], engines=[ENG.Pool], min_val=0, max_val=1,
                                      skip_runtime_bounds_check_because="the flag is clamped to 0..1")
            with pool.If(unsorted):
                pool.wait_ge(posd_made, 1)
                with pool.Fori(0, EC) as c:
                    nc.gpsimd.tensor_copy(idx_slot[:, :], pos_i[:, ds(c, 1)])
                    nc.gpsimd.tensor_copy(rec_slot[:, :], rec[:, ds(c, 1), :].rearrange("p c f -> p (c f)")).then_inc(pstep, 1)
                    pool.wait_ge(pstep, steps.k + 1 + c)
                    pool.sem_inc(held, 1)
                    nc.gpsimd.indirect_dma_start(
                        out=rec_d[0:E, :], out_offset=bass.IndirectOffsetOnAxis(ap=idx_slot[:, 0:1], axis=0),
                        in_=rec_slot[:, :], in_offset=None, bounds_check=E - 1, oob_is_err=False).then_inc(slot_out, 16)
                    pool.wait_ge(slot_out, 16 * (c + 1))
                    pool.sem_inc(held, 1)
                pool.sem_inc(recs_out, 1)
            with pool.Else():
                rec_v = rec_d[0:E, :].rearrange("(p c) f -> p (c f)", p=EP)
                rec_s = rec[:, :, :].rearrange("p c f -> p (c f)")
                pool.dma_start(rec_v[0:FIRST, :], rec_s[0:FIRST, :]).then_inc(first_out, 16)
                pool.dma_start(rec_v[FIRST:EP, :], rec_s[FIRST:EP, :]).then_inc(slot_out, 16)
                pool.wait_ge(first_out, 16)
                pool.sem_inc(recs_out, 1)
                pool.wait_ge(slot_out, 16)
            nc.gpsimd.memset(rows_a[:, :, :, C_ONE], 1.0).then_inc(recs_out, 1)
            pool.wait_ge(recs_out, 2)

            @turns(pool, TURNS_A)
            def _(i):
                for k in range(HB):
                    pool.wait_ge(a_idx[k], i + 1)
                    pool.wait_ge(a_rows[k], i + 1)
                    pool.sem_inc(held, 1)
                    for j in range(GA):
                        nc.gpsimd.indirect_dma_start(
                            out=rows_d[0:E, :], out_offset=bass.IndirectOffsetOnAxis(ap=idx_a[:, k, j:j + 1], axis=0),
                            in_=rows_a[:, k, j, :], in_offset=None, bounds_check=E - 1,
                            oob_is_err=False).then_inc(a_sent[k], 16)

            def windows_of(first, groups):
                return entries(ENG.Pool, "s", 1, first * GB, groups * GB, NW - 1)

            def add_sums(i, k, w):
                pool.wait_ge(b_out[k % 2], HS // 2 * i + k // 2 + 1)
                since(pool, b_added[(k - 1) % 2], HS // 2 * i + (k + 1) // 2)
                pool.sem_inc(held, 1)
                for b in range(GB):
                    if b:
                        pool.wait_ge(b_half, (i * HS + k) * (GB - 1) + b)
                        pool.sem_inc(held, 1)
                    here = acc[:, ds(w[b], 1), :].rearrange("p o c -> p (o c)")
                    nc.gpsimd.tensor_tensor(here, here, sums_b[:, k % 2, b * ACC:(b + 1) * ACC], ALU.add).then_inc(
                        b_half if b < GB - 1 else b_added[k % 2], 1)

            def weigh(i, groups=HS):
                first = isinstance(i, int) and i == 0
                w = [None] * (3 * GB) + list(windows_of(0, HS - 3)) if first else windows_of(i * HS - 3, groups)
                for k in range(groups):
                    if k >= 3:
                        add_sums(i, k - 3, w[k * GB:(k + 1) * GB])
                    elif not first:
                        add_sums(i - 1, k + HS - 3, w[k * GB:(k + 1) * GB])
                    p, n = k % 2, HS // 2 * i + k // 2
                    slot, used = before2(k, i, HS)
                    since(pool, b_sum[slot], used)
                    pool.wait_ge(b_wg[p], n + 1)
                    pool.sem_inc(held, 1)
                    nc.gpsimd.tensor_scalar(cap_b[:, p, :], wg_b[:, p, :], TOP, None, ALU.min).then_inc(b_cap[p], 1)
                    pool.wait_ge(b_cap[p], n + 1)
                    nc.gpsimd.tensor_tensor(onew_b[:, p, :, :], one_a[:, k, :, :],
                                            cap_b[:, p, :].unsqueeze(2).to_broadcast([P, CB, P]),
                                            ALU.mult).then_inc(b_onew[k], 1)

            turns(pool, TURNS_B)(weigh)
            weigh(TURNS_B, REST_B)
            w = windows_of(GROUPS_B - 3, 3)
            for k in range(3):
                add_sums(TURNS_B, REST_B - 3 + k, w[k * GB:(k + 1) * GB])

            pool.wait_ge(rinv_made, 1)

            @turns(pool, NW // HR)
            def _(i):
                w = ds(i * HR, HR)
                nc.gpsimd.tensor_tensor(acc[:, w, 0:D], acc[:, w, 0:D],
                                        rinv[:, w].unsqueeze(2).to_broadcast([P, HR, D]), ALU.mult).then_inc(z_ready, 1)

            for t in range(HR):
                pool.wait_ge(msg_out[t], 16 * (NW // HR))
            @turns(pool, TURNS_C)
            def _(i):
                for g in range(HC):
                    pool.wait_ge(c_rec[g], 16 * GC * (i + 1))
                    since(pool, c_sum[g], i)
                    pool.sem_inc(held, 1)
                    for j in range(GC):
                        nc.gpsimd.indirect_dma_start(
                            out=msg_c[:, g, j, :], out_offset=None, in_=msg_d[:, :],
                            in_offset=bass.IndirectOffsetOnAxis(ap=rec_c[:, g, j, F_MSG:F_MSG + 1].bitcast(I32), axis=0),
                            bounds_check=NW * P * R8 - 1, oob_is_err=False).then_inc(c_msg[g], 16)

        @block.vector
        def _(dve):
            v = nc.vector
            steps = Chain(dve, vstep)
            link = steps.link

            v.memset(xs[:, NW - 1, :], 0.0).then_inc(consts, 1)
            v.memset(ones[:, :], 1.0)
            v.memset(crow[:, :], 0.0)
            v.memset(rhs1[:, TC:TS], 0.0)
            v.memset(signs[:, NW:NW + 1], -float(EC))
            link(v.memset(falls[:, :], 0.0))
            dve.wait_ge(iotas, 4)
            v.tensor_scalar(halves[:, :], iota_c[0:EP, 0:NW], -1.0, 0.5, ALU.mult, ALU.add).then_inc(halves_made, 1)
            v.tensor_scalar(before[:, :], iota_c[:, :], iota_p[:, 0:1], None, ALU.is_gt)
            v.tensor_scalar(ident[:, :], iota_c[:, :], iota_p[:, 0:1], None, ALU.is_equal)
            v.tensor_scalar(identb[:, :], iota_c[:, :], iota_p[:, 0:1], None, ALU.is_equal)
            v.tensor_copy(iota_cb[:, :], iota_c[:, :]).then_inc(consts, 1)

            dve.wait_ge(edges_in, 16 * 5)
            link(v.tensor_scalar(hi_i[:, :], edge_i["dst"][:, :], 7, None, ALU.arith_shift_right))
            v.tensor_copy(hi["dst"][:, :], hi_i[:, :]).then_inc(hi_made, 1)
            dve.wait_ge(hi_made, 1)
            link(v.tensor_scalar(hi_i[:, :], edge_i["src"][:, :], 7, None, ALU.arith_shift_right))
            link(v.tensor_copy(hi["src"][:, :], hi_i[:, :]))
            link(v.tensor_tensor(mask[0][:, 0:EC - 1], hi["dst"][:, 0:EC - 1], hi["dst"][:, 1:EC], ALU.is_gt))
            link(v.tensor_reduce(falls[:, 0:1], mask[0][:, 0:EC - 1], mybir.AxisListType.X, ALU.add))
            link(v.tensor_scalar(nexthi[0:EP - 1, :], nexthi[0:EP - 1, :], 7, None, ALU.arith_shift_right))
            link(v.tensor_copy(nexthif[0:EP - 1, :], nexthi[0:EP - 1, :]))
            link(v.tensor_tensor(falls[0:EP - 1, 1:2], hi["dst"][0:EP - 1, EC - 1:EC], nexthif[0:EP - 1, :], ALU.is_gt))
            link(v.tensor_tensor(fall[:, :], falls[:, 0:1], falls[:, 1:2], ALU.add))
            with dve.Fori(0, NW // HR) as i:
                steps.turn(i, 1, 0)
                for t in range(HR):
                    last = v.tensor_scalar(unread[t], hi["src"][:, :], iota_c[0:EP, ds(i * HR + t, 1)], 0.0,
                                           ALU.is_equal, ALU.add, accum_out=cnt["src"][:, ds(i * HR + t, 1)])
                link(last)
            steps.end(NW // HR)
            dve.wait_ge(theta_done, 1)
            link(v.tensor_scalar(th[:, :], bank[3][:, 0:R], b2_sb[:, 0:1], None, ALU.add))
            link(v.tensor_scalar(whole[:, :], th[:, :], 0.15915494309189535, 0.25, ALU.mult, ALU.add))
            link(v.tensor_scalar(whole[:, :], whole[:, :], ROUND, None, ALU.add))
            link(v.tensor_scalar(whole[:, :], whole[:, :], ROUND, None, ALU.subtract))
            for part_of in (TWO_PI_A, TWO_PI_B, TWO_PI_C):
                link(v.scalar_tensor_tensor(th[:, :], whole[:, :], -part_of, th[:, :], ALU.mult, ALU.add))
            link(v.tensor_scalar(th[:, :], th[:, :], 1.5707963267948966, PI, ALU.add, ALU.min))
            v.tensor_scalar(th[:, :], th[:, :], -PI, None, ALU.max).then_inc(angle, 1)
            dve.wait_ge(x_in, 32)
            with dve.Fori(0, NW // HR) as i:
                steps.turn(i, 1, 0)
                for t in range(HR):
                    last = v.bn_stats(stats[:, ds(i * HR + t, 1), :].rearrange("p o s -> p (o s)"),
                                      xs[:, ds(i * HR + t, 1), :].rearrange("p o d -> p (o d)"))
                link(last)
            steps.end(NW // HR)
            def variances():
                even_m, even_v, odd_m, odd_v = (stats[:, :, c] for c in (1, 2, 4, 5))
                link(v.tensor_tensor(ln_d[:, :], even_m, odd_m, ALU.subtract))
                link(v.tensor_tensor(ln_m[:, :], even_m, odd_m, ALU.add))
                link(v.tensor_tensor(ln_v[:, :], even_v, odd_v, ALU.add))
                link(v.scalar_tensor_tensor(ln_d[:, :], ln_d[:, :], 0.25, ln_d[:, :], ALU.mult, ALU.mult))
                link(v.scalar_tensor_tensor(ln_v[:, :], ln_v[:, :], 1.0 / D, ln_d[:, :], ALU.mult, ALU.add))
                v.tensor_scalar(ln_v[:, :], ln_v[:, :], 1e-5, None, ALU.add).then_inc(var_ready, 1)

            def scales(n):
                dve.wait_ge(std_ready, n)
                link(v.reciprocal(ln_r[:, :], ln_d[:, :]))
                v.scalar_tensor_tensor(ln_b[:, :], ln_m[:, :], -0.5, ln_r[:, :], ALU.mult, ALU.mult).then_inc(ln_ready, 1)

            variances()
            dve.wait_ge(signs_made, NW // HR)
            link(v.tensor_tensor(cnt["dst"][:, :], signs[:, 0:NW], signs[:, 1:NW + 1], ALU.subtract))
            v.tensor_scalar(cnt["dst"][:, :], cnt["dst"][:, :], 0.5, None, ALU.mult).then_inc(counted, 1)
            v.tensor_copy(rec[:, :, F_DST], edge_i["dst"][:, :])
            v.tensor_copy(rec[:, :, F_SRC], edge_i["src"][:, :])
            v.tensor_copy(rec[:, :, F_TYPE], edge_i["t100"][:, :])
            v.scalar_tensor_tensor(rec[:, :, F_MSG].bitcast(I32), edge_i["src"][:, :], float(R8), edge_i["t8"][:, :],
                                   ALU.mult, ALU.add)
            dve.wait_ge(totals, 1)
            for n, k in enumerate(("dst", "src")):
                link(v.tensor_copy(tot[k][:, :], bank[n][:, 0:NW]))
                link(v.tensor_tensor_scan(upto[k][:, :], tot[k][:, :], tot[k][:, :], 0.0, ALU.add, ALU.bypass))
                link(v.tensor_tensor(junkw[:, :], upto[k][:, :], tot[k][:, :], ALU.subtract))
                link(v.tensor_tensor(base[k][:, :], bank[n][0:EP, 64:64 + NW], junkw[0:EP, :], ALU.add))
            v.tensor_scalar(unsorted_i[:, :], bank[0][0:1, 128:129], 1.0, None, ALU.min).then_inc(flag_i, 1)
            for n, (s, k, size, kk, off) in enumerate((("d", "dst", P, KD, 0), ("s", "src", P * QB, KS, KD))):
                if n:
                    dve.wait_ge(table_out, 32)
                link(v.tensor_scalar(nblk_i[:, :], tot[k][:, :], float(size - 1), None, ALU.add))
                link(v.tensor_scalar(nblk_i[:, :], nblk_i[:, :], size.bit_length() - 1, None, ALU.arith_shift_right))
                link(v.tensor_copy(nblk[:, :], nblk_i[:, :]))
                link(v.tensor_tensor_scan(cumblk[:, :], nblk[:, :], nblk[:, :], 0.0, ALU.add, ALU.bypass))
                link(v.scalar_tensor_tensor(padded[:, :], nblk[:, :], float(size), tot[k][:, :], ALU.mult, ALU.subtract))
                for c in range(kk):
                    number = chunk_no[:, off + c:off + c + 1]
                    link(v.tensor_scalar(junkw[:, :], cumblk[:, :], number, 0.0, ALU.is_le, ALU.add,
                                         accum_out=wcol[:, c:c + 1]))
                    link(v.scalar_tensor_tensor(junkw[:, :], cumblk[:, :], number, padded[:, :], ALU.is_le, ALU.mult,
                                                accum_out=ocol[:, c:c + 1]))
                link(v.scalar_tensor_tensor(ocol[:, 0:kk], chunk_no[:, off:off + kk], float(size), ocol[:, 0:kk],
                                            ALU.mult, ALU.subtract))
                link(v.tensor_scalar(wcol[:, 0:kk], wcol[:, 0:kk], float(NW - 1), None, ALU.min))
                v.tensor_scalar(w128[:, 0:kk], wcol[:, 0:kk], float(P), None, ALU.mult)
                v.tensor_copy(wo_i[:, 1, 0:kk], wcol[:, 0:kk])
                v.tensor_scalar(wo_i[:, 0, 0:kk], ocol[:, 0:kk], float(E), None, ALU.min).then_inc(table_made, 1)

            v.tensor_copy(rhs1[:, 0:D], wsb[:, 0, :])
            v.tensor_copy(rhs1[:, 128:129], wa[:, 1:2])
            v.tensor_copy(crow[:, 128:129], bank[3][0:1, 128:129])
            dve.wait_ge(cosine, 1)
            v.tensor_scalar(rhs1[:, T_S:TC], whole[:, :], wa[:, 2:3], wa[:, 0:1], ALU.mult, ALU.add).then_inc(rhs_ready, 1)

            scales(1)
            @turns(dve, NW // HR)
            def _(i):
                def mark(t):
                    return steps.put(v.tensor_scalar(mask[t % 2], hi["src"][:, :], iota_c[0:EP, ds(i * HR + t, 1)], None,
                                                     ALU.is_equal))

                def scan(t, marked):
                    steps.after(marked)
                    return steps.put(v.tensor_tensor_scan(rank[:, :], mask[t % 2], mask[t % 2],
                                                          base["src"][:, ds(i * HR + t, 1)], ALU.add, ALU.max))

                def pick(t, scanned):
                    since(dve, part_added, i * HR + max(t - 1, 0))
                    steps.after(scanned)
                    v.tensor_tensor(part[t % 2][:, :], mask[t % 2], rank[:, :], ALU.mult).then_inc(part_made, 1)

                def middle(t):
                    dve.wait_ge(high, i * HR + t + 1)
                    since(dve, low, i * HR + t + 1 - HR)
                    v.tensor_tensor(rest[:, t, 0:TC], bank[2 + t % 4][:, 0:TC], part_of_table(i * HR + t, 0),
                                    ALU.subtract).then_inc(rest_mid, 1)

                steps.turn(i, 2 * HR)
                since(dve, part_made, i * HR)
                marked = mark(0)
                for t in range(HR):
                    if t:
                        dve.wait_ge(part_made, i * HR + t)
                    scanned = scan(t, marked)
                    if t < HR - 1:
                        marked = mark(t + 1)
                    pick(t, scanned)
                    if t:
                        middle(t - 1)
                middle(HR - 1)
            steps.end(NW // HR)

            dve.wait_ge(part_added, NW)
            v.tensor_copy(rec[:, :, F_POS], pos["src"][:, :]).then_inc(recs_made, 1)
            dve.wait_ge(flag_i, 1)
            unsorted = nc.values_load(unsorted_i[0:1, 0:1], engines=[ENG.DVE], min_val=0, max_val=1,
                                      skip_runtime_bounds_check_because="the flag is clamped to 0..1")
            with dve.If(unsorted):
                dve.wait_ge(low, NW)
                v.memset(pos["dst"][:, :], -1.0).then_inc(posd_cleared, 1)
                dve.wait_ge(posd_cleared, 1)
                with dve.Fori(0, NW) as b:
                    for t, make in enumerate((
                            lambda: v.tensor_scalar(mask[0][:, :], hi["dst"][:, :], iota_c[0:EP, ds(b, 1)], None, ALU.is_equal),
                            lambda: v.tensor_tensor_scan(rank[:, :], mask[0][:, :], mask[0][:, :], base["dst"][:, ds(b, 1)],
                                                         ALU.add, ALU.max),
                            lambda: v.tensor_tensor(part[0][:, :], mask[0][:, :], rank[:, :], ALU.mult),
                            lambda: v.tensor_tensor(pos["dst"][:, :], pos["dst"][:, :], part[0][:, :], ALU.add))):
                        make().then_inc(posd_step, 1)
                        dve.wait_ge(posd_step, 4 * b + t + 1)
                v.tensor_copy(pos_i[:, :], pos["dst"][:, :]).then_inc(posd_made, 1)

            dve.wait_ge(tables, 64)
            @turns(dve, TURNS_A)
            def _(i):
                steps.turn(i, 3 * HB)
                for k in range(HB):
                    p, n = k % 2, 2 * i + k // 2
                    dve.wait_ge(a_rec[k], 16 * GA * (i + 1))
                    link(v.tensor_tensor(rel_a[:, p, :], rec_a[:, k, :, F_DST],
                                         tab_w["d"][:, ds((i * HB + k) * GA, GA)], ALU.subtract))
                    since(dve, a_turned[p], n)
                    for j in range(GA):
                        last = v.tensor_scalar(one_a[:, p, j, :], iota_cb[:, :], rel_a[:, p, j:j + 1], None, ALU.is_equal)
                    last.then_inc(a_one[p], 1)
                    link(v.scalar_tensor_tensor(q_a[:, p, :], rel_a[:, p, :], -127.0, rel_a[:, p, :], ALU.add, ALU.mult))
                    link(v.tensor_scalar(m_a[:, p, :], q_a[:, p, :], 0.0, OUT, ALU.is_gt, ALU.mult))
                    since(dve, a_sent[k], 16 * GA * i)
                    v.tensor_copy(rows_a[:, k, :, C_SRC:ROW], rec_a[:, k, :, F_SRC:F_TYPE + 1])
                    v.tensor_tensor(idx_a[:, k, :], m_a[:, p, :], rec_a[:, k, :, F_POS], ALU.add).then_inc(a_idx[k], 1)
            steps.end(TURNS_A)

            dve.wait_ge(recs_out, 2)
            v.memset(acc[:, :, :], 0.0)

            def one_hot(i, k):
                p, n = k % 2, HS // 2 * i + k // 2
                dve.wait_ge(b_rel[p], n + 1)
                since(dve, b_onew[k], i)
                v.tensor_tensor(one_a[:, k, :, :], iota_cb[:, :].unsqueeze(1).to_broadcast([P, CB, P]),
                                rel_b[:, p, :, :].rearrange("p b q -> p (b q)").unsqueeze(2).to_broadcast([P, CB, P]),
                                ALU.is_equal).then_inc(b_one[p], 1)

            def score(i, k):
                p, n = k % 2, HS // 2 * i + k // 2
                dve.wait_ge(b_got[p], n + 1)
                since(dve, b_wg[p], n)
                for s in range(CB):
                    last = v.scalar_tensor_tensor(junk_b[:, s, :], iota_c[:, 0:R], rows_b[:, k, s // QB, s % QB, C_TYPE:ROW],
                                                  bank[2 + 2 * p + s // 4][:, (s % 4) * R:(s % 4 + 1) * R],
                                                  ALU.is_equal, ALU.mult, accum_out=sel_b[:, p, s:s + 1])
                link(last)
                link(v.tensor_tensor(sc_b[:, p, :], sel_b[:, p, :],
                                     rows_b[:, k, :, :, C_A3].rearrange("p b q -> p (b q)"), ALU.add))
                v.scalar_tensor_tensor(lr_b[:, p, :], sc_b[:, p, :], 0.2, sc_b[:, p, :], ALU.mult, ALU.max).then_inc(b_lr[p], 1)

            one_hot(0, 0)

            def scores(i, groups=HS):
                steps.turn(i, HS * 2)
                for k in range(groups):
                    one_hot(i + (k + 1) // HS, (k + 1) % HS)
                    score(i, k)
            turns(dve, TURNS_B)(scores)
            steps.end(TURNS_B)
            scores(TURNS_B, REST_B)
            dve.wait_ge(b_added[(REST_B - 1) % 2], HS // 2 * TURNS_B + (REST_B - 1) // 2 + 1)

            link(v.tensor_scalar(ln_d[:, :], acc[:, :, C_ONE], 0.0, 1e-12, ALU.is_equal, ALU.mult))
            link(v.tensor_tensor(ln_d[:, :], ln_d[:, :], acc[:, :, C_ONE], ALU.add))
            v.reciprocal(rinv[:, :], ln_d[:, :]).then_inc(rinv_made, 1)
            @turns(dve, NW // HR)
            def _(i):
                steps.turn(i, 4)
                w = ds(i * HR, HR)
                since(dve, x_kept, i)
                dve.wait_ge(z_ready, i + 1)
                link(v.scalar_tensor_tensor(xn[:, :, :], acc[:, w, 0:D], 0.0, xs[:, w, :], ALU.max, ALU.add))
                dve.wait_ge(z_exp, i + 1)
                link(v.scalar_tensor_tensor(xn[:, :, :], ez[:, :, :], -1.0, xn[:, :, :], ALU.add, ALU.add))
                v.sem_inc(x_new, 1)
                for t in range(HR):
                    bn = v.bn_stats(xn_stats[:, t, :], xn[:, t, :])
                link(bn)
                link(v.tensor_copy(stats[:, w, :], xn_stats[:, :, :]))
            steps.end(NW // HR)
            variances()
            scales(2)
            def copy_features(i, t):
                dve.wait_ge(h_turned, NW + i * HR + t + 1)
                v.tensor_copy(hT[:, t, :], bank[t % 2][:, 0:P]).then_inc(hT_ready, 1)

            def messages(i, last=False):
                for t in range(HR):
                    if t < HR - 1:
                        copy_features(i, t + 1)
                    elif not last:
                        copy_features(i + 1, 0)
                    dve.wait_ge(msg_done, i * HR + t + 1)
                    since(dve, msg_out[t], 16 * i)
                    for c in range(2):
                        half = v.tensor_tensor(
                            msg_o[:, t, c * 512:(c + 1) * 512].rearrange("p (r d) -> p r d", d=D),
                            bank[2 + 2 * MSG_BANKS[t] + c][:, :].rearrange("p (r d) -> p r d", d=D),
                            bias_sb[:, :].unsqueeze(1).to_broadcast([P, 4, D]), ALU.add)
                    half.then_inc(msg_sum, 1)

            copy_features(0, 0)
            turns(dve, NW // HR - 1)(messages)
            messages(NW // HR - 1, True)

            @turns(dve, TURNS_C)
            def _(i):
                steps.turn(i, HC * (1 + GC))
                for g in range(HC):
                    dve.wait_ge(c_rec[g], 16 * GC * (i + 1))
                    link(v.tensor_tensor(rel_c[:, g, :], rec_c[:, g, :, F_DST],
                                         tab_w["d"][:, ds(i * (GC * HC) + g * GC, GC)], ALU.subtract))
                    since(dve, c_sum[g], i)
                    for j in range(GC):
                        last = v.tensor_scalar(one_c[:, g, j, :], iota_c[:, :], rel_c[:, g, j:j + 1], None, ALU.is_equal)
                    last.then_inc(c_one[g], 1)
                for g in range(HC):
                    w = entries(ENG.DVE, "d", 1, i * (GC * HC) + g * GC, GC, NW - 1)
                    dve.wait_ge(c_sum[g], i + 1)
                    for j in range(GC):
                        here = xs[:, ds(w[j], 1), :].rearrange("p o d -> p (o d)")
                        link(v.tensor_tensor(here, here, bank[g][:, j * D:(j + 1) * D], ALU.add))
                    v.sem_inc(c_added[g], 1)
            steps.end(TURNS_C)
            v.sem_inc(x_done, 1)

        @block.scalar
        def _(act):
            s = nc.scalar
            act.wait_ge(halves_made, 1)
            act.wait_ge(hi_made, 1)

            def count_signs(i):
                since(act, signs_made, i)
                for t in range(HR):
                    last = s.activation(signs_out[:, t, :], hi["dst"][:, :], ACT.Sign, bias=halves[:, ds(i * HR + t, 1)],
                                        accum_out=signs[:, ds(i * HR + t, 1)])
                last.then_inc(signs_made, 1)

            count_signs(0)
            act.wait_ge(weightsT, 1)
            s.copy(wT[:, :], bank[4][:, 0:2 * P + R]).then_inc(wT_copied, 1)
            act.wait_ge(hid_done, 1)
            for k in range(HK):
                s.activation(hidT[:, k, :], bank[5][:, k * R:(k + 1) * R], ACT.Relu, bias=b1_sb[:, k:k + 1])
            s.copy(wa[:, :], bank[6][:, 0:3]).then_inc(hid_copied, 1)
            with act.Fori(1, NW // HR) as i:
                count_signs(i)

            act.wait_ge(angle, 1)
            s.activation(whole[:, :], th[:, :], ACT.Sin).then_inc(cosine, 1)

            def norm_turn(n, t, i):
                since(act, h_turned, (n - 1) * NW + i * HR + t + 1 - HR)
                w = i * HR + t
                s.activation(h_t[:, t, :], xs[:, ds(w, 1), :].rearrange("p o d -> p (o d)"), ACT.Relu,
                             bias=ln_b[:, ds(w, 1)], scale=ln_r[:, ds(w, 1)]).then_inc(h_ready, 1)

            act.wait_ge(var_ready, 1)
            s.activation(ln_d[:, :], ln_v[:, :], ACT.Sqrt).then_inc(std_ready, 1)
            act.wait_ge(ln_ready, 1)
            act.wait_ge(tails_out, 32)
            @turns(act, NW // HR)
            def _(i):
                for t in range(HR):
                    norm_turn(1, t, i)
                for t in range(HR + 2):
                    if t < HR:
                        act.wait_ge(h_turned, i * HR + t + 1)
                        s.copy(hT[:, t, :], bank[t % 2][:, 0:P]).then_inc(hT_ready, 1)
                    if 1 <= t <= HR:
                        act.wait_ge(dense, i * HR + t)
                        s.copy(part_of_table(i * HR + t - 1, 0), bank[2 + (t - 1) % 4][:, 0:TC]).then_inc(high, 1)
                    if t >= 2:
                        act.wait_ge(rest_mid, i * HR + t - 1)
                        s.copy(part_of_table(i * HR + t - 2, 1), rest[:, t - 2, 0:TC]).then_inc(mid, 1)

            act.wait_ge(low, NW)
            def copy_turned(turned, got, ready, p, n, chunks):
                act.wait_ge(turned[p], n + 1)
                since(act, got[p], n)
                s.copy(oneT_a[:, p, 0:chunks, :].rearrange("p j e -> p (j e)"),
                       bank[p][:, :].bitcast(BF16)[:, 0:chunks * P]).then_inc(ready[p], 1)

            @turns(act, TURNS_A)
            def _(i):
                for pair in range(0, HB, 2):
                    for k in (pair, pair + 1):
                        copy_turned(a_turned, a_got, a_oneT, k % 2, 2 * i + k // 2, GA)
                    for k in (pair, pair + 1):
                        p, n = k % 2, 2 * i + k // 2
                        act.wait_ge(a_got[p], n + 1)
                        since(act, a_sent[k], 16 * GA * i)
                        for b in range(2):
                            last = s.copy(rows_a[:, k, 2 * b:2 * b + 2, 0:T_S],
                                          bank[2 + 2 * p + b][:, 0:2 * T_S].rearrange("p (j c) -> p j c", j=2))
                        last.then_inc(a_rows[k], 1)

            def relative(i, k, windows):
                p, n = k % 2, HS // 2 * i + k // 2
                act.wait_ge(b_rows[k], 16 * GB * (i + 1))
                since(act, b_one[p], n)
                for b in range(GB):
                    last = s.activation(rel_b[:, p, b, :], rows_b[:, k, b, :, C_SRC], ACT.Identity,
                                        bias=windows[:, b:b + 1])
                last.then_inc(b_rel[p], 1)

            def near_windows(first, groups, turn):
                s.mul(near_b[:, 0:groups * GB], tab_w["s"][:, ds(first * GB, groups * GB)], -1.0).then_inc(b_near, 1)
                act.wait_ge(b_near, turn)

            near_windows(0, 2, 1)
            for k in range(2):
                relative(0, k, near_b[:, k * GB:(k + 1) * GB])
            copy_turned(b_turned, b_got, b_oneT, 0, 0, CB)

            def sums_out(i, k):
                p, n = k % 2, HS // 2 * i + k // 2
                act.wait_ge(b_sum[k], i + 1)
                since(act, b_added[p], n)
                s.copy(sums_b[:, p, :], bank[6 + p][:, 0:GB * ACC]).then_inc(b_out[p], 1)

            def weights(i, groups=HS):
                act.wait_ge(b_rel[1], HS // 2 * i + 1)
                near_windows(i * HS + 2, groups, i + 2)
                for k in range(groups):
                    if k >= 3:
                        sums_out(i, k - 3)
                    elif not (isinstance(i, int) and i == 0):
                        sums_out(i - 1, k + HS - 3)
                    relative(i + (k + 2) // HS, (k + 2) % HS, near_b[:, k * GB:(k + 1) * GB])
                    copy_turned(b_turned, b_got, b_oneT, (k + 1) % 2, HS // 2 * i + (k + 1) // 2, CB)
                    p, n = k % 2, HS // 2 * i + k // 2
                    act.wait_ge(b_lr[p], n + 1)
                    since(act, b_cap[p], n)
                    s.activation(wg_b[:, p, :], lr_b[:, p, :], ACT.Exp, scale=-1.0).then_inc(b_wg[p], 1)
            turns(act, TURNS_B)(weights)
            weights(TURNS_B, REST_B)
            for k in range(REST_B - 3, REST_B):
                sums_out(TURNS_B, k)

            @turns(act, NW // HR)
            def _(i):
                act.wait_ge(z_ready, i + 1)
                since(act, x_new, i)
                s.activation(ez[:, :, :], acc[:, ds(i * HR, HR), 0:D], ACT.Relu, scale=-1.0).then_inc(z_down, 1)
                act.wait_ge(z_down, i + 1)
                s.activation(ez[:, :, :], ez[:, :, :], ACT.Exp, scale=-1.0).then_inc(z_exp, 1)
                act.wait_ge(x_new, i + 1)
                s.copy(xs[:, ds(i * HR, HR), :], xn[:, :, :]).then_inc(x_kept, 1)
            act.wait_ge(var_ready, 2)
            s.activation(ln_d[:, :], ln_v[:, :], ACT.Sqrt).then_inc(std_ready, 1)
            act.wait_ge(ln_ready, 2)
            for t in range(HR):
                norm_turn(2, t, 0)

            def messages(i, last=False):
                for t in range(HR):
                    act.wait_ge(msg_sum, i * HR + t + 1)
                    s.activation(msg_o[:, t, :], msg_o[:, t, :], ACT.Relu).then_inc(msg_ready, 1)
                    if not last:
                        norm_turn(2, t, i + 1)
            turns(act, NW // HR - 1)(messages)
            messages(NW // HR - 1, True)

        @block.tensor
        def _(pe):
            t_ = nc.tensor

            def mm(o, l, r, start=True, stop=True):
                return t_.matmul(o, l, r, start=start, stop=stop)

            pe.wait_ge(consts, 2)
            pe.wait_ge(weights_in, 16 * 11)
            t_.transpose(bank[4][:, 0:P], wsb[:, 0, :], ident[:, :])
            t_.transpose(bank[4][:, P:2 * P], wsb[:, 1, :], ident[:, :])
            t_.transpose(bank[4][:, 2 * P:2 * P + R], emb_sb[:, :], ident[0:R, 0:R]).then_inc(weightsT, 1)
            pe.wait_ge(wT_copied, 1)
            embT = wT[:, 2 * P:2 * P + R]
            for k in range(HK):
                mm(bank[5][:, k * R:(k + 1) * R], w1_sb[:, k * P:(k + 1) * P], embT)
            mm(bank[6][:, 0:1], wT[:, 0:P], a_sb[:, 0:1])
            mm(bank[6][:, 1:2], wT[:, 0:P], a_sb[:, 2:3])
            mm(bank[6][:, 2:3], wT[:, P:2 * P], a_sb[:, 1:2]).then_inc(hid_done, 1)
            pe.wait_ge(hid_copied, 1)
            for k in range(HK):
                mm(bank[3][:, 0:R], w2_sb[:, k, :], hidT[:, k, :], k == 0, k == HK - 1)
            mm(bank[3][0:1, 128:129], cr_sb[:, :], wa[:, 2:3]).then_inc(theta_done, 1)
            pe.wait_ge(counted, 1)
            for n, k in enumerate(("dst", "src")):
                mm(bank[n][:, 0:NW], ones[0:EP, :], cnt[k][:, :])
                mm(bank[n][0:EP, 64:64 + NW], before[0:EP, 0:EP], cnt[k][:, :])
            mm(bank[0][0:1, 128:129], fall[:, :], ones[0:EP, 0:1]).then_inc(totals, 1)

            pe.wait_ge(rhs_ready, 1)
            pe.wait_ge(flag_i, 1)
            def turn_features(n, i, t):
                done = (n - 1) * NW + i * HR
                pe.wait_ge(h_ready, done + t + 1)
                since(pe, hT_ready, done + max(t - 1, 0))
                t_.transpose(bank[t % 2][:, 0:P], h_t[:, t, :], ident[:, :]).then_inc(h_turned, 1)

            @turns(pe, NW // HR)
            def _(i):
                for t in range(HR + 1):
                    if t < HR:
                        turn_features(1, i, t)
                    if t >= 1:
                        pe.wait_ge(hT_ready, i * HR + t)
                        since(pe, rest_mid, i * HR + max(t - 4, 0))
                        to = bank[2 + (t - 1) % 4][:, 0:TC]
                        mm(to, hT[:, t - 1, :], rhs1[:, 0:TC], True, False)
                        mm(to, ones[0:1, :], crow[:, 0:TC], False, True).then_inc(dense, 1)

            pe.wait_ge(low, NW)
            pe.wait_ge(tables, 64)
            def turn_one_hot(one, ready, turned, slot, p, n, chunks):
                pe.wait_ge(one[p], n + 1)
                since(pe, ready[p], n)
                for j in range(chunks):
                    last = t_.transpose(bank[p][:, :].bitcast(BF16)[:, j * P:(j + 1) * P], one_a[:, slot, j, :], identb[:, :])
                last.then_inc(turned[p], 1)

            @turns(pe, TURNS_A)
            def _(i):
                for pair in range(0, HB, 2):
                    for k in (pair, pair + 1):
                        turn_one_hot(a_one, a_oneT, a_turned, k % 2, k % 2, 2 * i + k // 2, GA)
                    for k in (pair, pair + 1):
                        p, n = k % 2, 2 * i + k // 2
                        w = entries(ENG.PE, "d", 1, (i * HB + k) * GA, GA, NW - 1)
                        pe.wait_ge(a_oneT[p], n + 1)
                        slot, used = before2(k, i)
                        since(pe, a_rows[slot], used)
                        for j in range(GA):
                            to = bank[2 + 2 * p + j // 2][:, (j % 2) * T_S:(j % 2 + 1) * T_S]
                            for c in range(3):
                                last = mm(to, oneT_a[:, p, j, :], table[:, ds(w[j], 1), c, 0:T_S].rearrange(
                                    "p o c -> p (o c)"), c == 0, c == 2)
                        last.then_inc(a_got[p], 1)

            def src_scores(i, k):
                p, n = k % 2, HS // 2 * i + k // 2
                w = entries(ENG.PE, "s", 1, (i * HS + k) * GB, GB, NW - 1)
                pe.wait_ge(b_oneT[p], n + 1)
                since(pe, b_lr[p], n)
                for j in range(CB):
                    to = bank[2 + 2 * p + j // 4][:, (j % 4) * R:(j % 4 + 1) * R]
                    for c in range(3):
                        last = mm(to, oneT_a[:, p, j, :],
                                  table[:, ds(w[j // QB], 1), c, T_S:TC].rearrange("p o c -> p (o c)"), c == 0, c == 2)
                last.then_inc(b_got[p], 1)

            def weighted_sums(i, k):
                p, n = k % 2, HS // 2 * i + k // 2
                pe.wait_ge(b_onew[k], i + 1)
                since(pe, b_out[p], n)
                for b in range(GB):
                    for q in range(QB):
                        last = mm(bank[6 + p][:, b * ACC:(b + 1) * ACC], onew_b[:, p, b * QB + q, :],
                                  rows_b[:, k, b, q, 0:ACC], q == 0, q == QB - 1)
                last.then_inc(b_sum[k], 1)

            turn_one_hot(b_one, b_oneT, b_turned, 0, 0, 0, CB)

            def products(i, groups=HS):
                for k in range(groups):
                    src_scores(i, k)
                    turn_one_hot(b_one, b_oneT, b_turned, (k + 1) % HS, (k + 1) % 2, HS // 2 * i + (k + 1) // 2, CB)
                    if k >= 2:
                        weighted_sums(i, k - 2)
                    elif not (isinstance(i, int) and i == 0):
                        weighted_sums(i - 1, k + HS - 2)
            turns(pe, TURNS_B)(products)
            products(TURNS_B, REST_B)
            for k in range(REST_B - 2, REST_B):
                weighted_sums(TURNS_B, k)

            w8v = w8_sb[:, :, :].rearrange("p r n -> p (r n)")
            def messages(i, last=False):
                for t in range(HR):
                    if t < HR - 1:
                        turn_features(2, i, t + 1)
                    elif not last:
                        turn_features(2, i + 1, 0)
                    pe.wait_ge(hT_ready, NW + i * HR + t + 1)
                    users = [u for u in range(t - HR, t) if MSG_BANKS[u] == MSG_BANKS[t]]
                    since(pe, msg_sum, i * HR + users[-1] + 1)
                    for c in range(2):
                        half = mm(bank[2 + 2 * MSG_BANKS[t] + c][:, :], hT[:, t, :], w8v[:, c * 512:(c + 1) * 512])
                    half.then_inc(msg_done, 1)

            turn_features(2, 0, 0)
            turns(pe, NW // HR - 1)(messages)
            messages(NW // HR - 1, True)

            pe.wait_ge(msg_sum, NW)
            @turns(pe, TURNS_C)
            def _(i):
                for g in range(HC):
                    pe.wait_ge(c_one[g], i + 1)
                    pe.wait_ge(c_msg[g], 16 * GC * (i + 1))
                    since(pe, c_added[g], i)
                    for j in range(GC):
                        last = mm(bank[g][:, j * D:(j + 1) * D], one_c[:, g, j, :], msg_c[:, g, j, :])
                    last.then_inc(c_sum[g], 1)


_INS = ['x', 'src', 'dst', 'edge_type_100', 'edge_type_8', 'L0_gnn_relation_embeds', 'L0_gnn_mlp_w1', 'L0_gnn_mlp_b1',
        'L0_gnn_mlp_w2', 'L0_gnn_mlp_b2', 'L0_gnn_c_r', 'L0_gnn_W', 'L0_gnn_W_r', 'L0_gnn_a', 'L1_gnn_weight',
        'L1_gnn_bias']


def kernel(**inputs):
    import numpy as _np
    import concourse.bacc as _bacc
    from concourse import mybir as _mybir
    from concourse.bass_utils import run_bass_kernel_spmd as _run

    nc = _bacc.Bacc("TRN2", target_bir_lowering=False, num_devices=1)
    arrays, args = {}, []
    for name in _INS:
        a = _np.ascontiguousarray(inputs[name])
        arrays[f"in_{name}"] = a
        args.append(nc.dram_tensor(f"in_{name}", a.shape, _mybir.dt.from_np(a.dtype), kind="ExternalInput").ap())
    out = nc.dram_tensor("out_x", (N, D), F32, kind="ExternalOutput").ap()
    build(nc, *args, out)
    r = _run(nc, [arrays], core_ids=[0])
    return r.results[0]["out_x"]
```
